# Optimizing a Trainium2 kernel written in Bass

```python
import numpy as np
import jax
import jax.numpy as jnp

def _softmax(x, axis=-1):
    return jax.nn.softmax(x, axis=axis)

def _gelu(x):
    return jax.nn.gelu(x, approximate=True)

def _silu(x):
    return jax.nn.silu(x)

def _sigmoid(x):
    return jax.nn.sigmoid(x)

def _layernorm(x, axis=-1, eps=1e-05):
    m = jnp.mean(x, axis=axis, keepdims=True)
    v = jnp.var(x, axis=axis, keepdims=True)
    return (x - m) / jnp.sqrt(v + eps)

def _scatter_add(tgt, idx, src, axis=0):
    return tgt.at[idx].add(src)

def _segment_sum(src, seg, n):
    return jax.ops.segment_sum(src, seg, n)
kernel_name = 'mk_xattn_ffn_d2_seqx_r8_41690d'

def setup_inputs(seed: int=0):
    np.random.seed(seed)
    _w = jnp.asarray

    def _rec_inputs():
        import jax
        import jax.numpy as jnp
        _rk = jax.random.key(seed)
        x = -0.000125 + 0.9999 * jax.random.normal(jax.random.fold_in(_rk, 1), (4, 256, 128), jnp.float32)
        _lenS = 256 - jax.random.randint(jax.random.fold_in(_rk, 7), (4,), 0, max(1, 256 // 4) + 1, jnp.int32)
        _lenS2 = 512 - jax.random.randint(jax.random.fold_in(_rk, 8), (4,), 0, max(1, 512 // 4) + 1, jnp.int32)
        _ctx_768P = jax.random.normal(jax.random.fold_in(_rk, 11), (4, 16, 96), jnp.float32)
        _ctx_768c = jax.random.dirichlet(jax.random.fold_in(_rk, 511), 0.3 * jnp.ones((16,), jnp.float32), (4, 512))
        _ctx_768t = jnp.einsum('bsk,bkd->bsd', _ctx_768c, _ctx_768P)
        _ctx_768t = _ctx_768t * jax.lax.rsqrt(jnp.mean(jnp.square(_ctx_768t)) + 1e-12) * 0.953939
        ctx_768 = 0.00272024 + 0.999456 * (_ctx_768t + 0.3 * jax.random.normal(jax.random.fold_in(_rk, 611), (4, 512, 96), jnp.float32))
        return (x, ctx_768)
    x, ctx_768 = _rec_inputs()

    def _L0_xattn_setup():
        import jax, jax.numpy as jnp
        import numpy as np
        QUERY_DIM = 128
        CONTEXT_DIM = 96
        HEADS = 8
        DIM_HEAD = 64
        INNER = HEADS * DIM_HEAD
        key = jax.random.key(seed)
        ks = jax.random.split(key, 7)
        B, S, L = (8, 512, 77)
        x = jax.random.normal(ks[0], (B, S, QUERY_DIM), dtype=jnp.float32)
        context = jax.random.normal(ks[1], (B, L, CONTEXT_DIM), dtype=jnp.float32)
        Wq = jax.random.normal(ks[2], (QUERY_DIM, INNER), dtype=jnp.float32) * QUERY_DIM ** (-0.5)
        Wk = jax.random.normal(ks[3], (CONTEXT_DIM, INNER), dtype=jnp.float32) * CONTEXT_DIM ** (-0.5)
        Wv = jax.random.normal(ks[4], (CONTEXT_DIM, INNER), dtype=jnp.float32) * CONTEXT_DIM ** (-0.5)
        Wo = jax.random.normal(ks[5], (INNER, QUERY_DIM), dtype=jnp.float32) * INNER ** (-0.5)
        bo = jax.random.normal(ks[6], (QUERY_DIM,), dtype=jnp.float32) * 0.01
        return {'x': x, 'context': context, 'Wq': Wq, 'Wk': Wk, 'Wv': Wv, 'Wo': Wo, 'bo': bo}
    _L0_xattn_all = _L0_xattn_setup()
    _L0_xattn_in = {k: v for k, v in _L0_xattn_all.items() if k in ('Wq', 'Wk', 'Wv', 'Wo', 'bo')}
    del _L0_xattn_all

    def _L0_ffn_setup():
        import jax, jax.numpy as jnp
        import numpy as np
        MANT_BITS = 8
        _PWL_X = jnp.linspace(-4.0, 4.0, 33, dtype=jnp.float32)
        _PWL_Y = 0.5 * _PWL_X * (1.0 + jax.lax.erf(_PWL_X / jnp.sqrt(jnp.float32(2.0))))

        def float2fix(x, mantissa_bits):
            s = jnp.float32(2.0 ** mantissa_bits)
            q = jnp.round(x * s) / s
            return x + jax.lax.stop_gradient(q - x)

        def pwlin_gelu_basic(x, mantissa_bits_in, mantissa_bits_out):
            xq = float2fix(x, mantissa_bits_in)
            y = jnp.interp(xq, _PWL_X, _PWL_Y)
            y = jnp.where(xq > 4.0, xq, jnp.where(xq < -4.0, jnp.float32(0.0), y))
            return float2fix(y, mantissa_bits_out)
        key = jax.random.key(seed)
        k_x, k_w1, k_b1, k_w2, k_b2 = jax.random.split(key, 5)
        dim, ff_dim = (128, 512)
        B, S = (32, 64)
        sc1 = 1.0 / np.sqrt(dim)
        sc2 = 1.0 / np.sqrt(ff_dim)
        return {'x': jax.random.normal(k_x, (B, S, dim), dtype=jnp.float32), 'w1': jax.random.uniform(k_w1, (dim, ff_dim), jnp.float32, -sc1, sc1), 'b1': jax.random.uniform(k_b1, (ff_dim,), jnp.float32, -sc1, sc1), 'w2': jax.random.uniform(k_w2, (ff_dim, dim), jnp.float32, -sc2, sc2), 'b2': jax.random.uniform(k_b2, (dim,), jnp.float32, -sc2, sc2)}
    _L0_ffn_all = _L0_ffn_setup()
    _L0_ffn_in = {k: v for k, v in _L0_ffn_all.items() if k in ('w1', 'b1', 'w2', 'b2')}
    del _L0_ffn_all

    def _L1_xattn_setup():
        import jax, jax.numpy as jnp
        import numpy as np
        IMAGE_DIM = 128
        TEXT_DIM = 96
        NUM_HEADS = 16
        HEAD_DIM = IMAGE_DIM // NUM_HEADS
        key = jax.random.key(seed)
        ks = jax.random.split(key, 14)
        B, N, M = (4, 512, 64)
        s_img = 1.0 / np.sqrt(IMAGE_DIM)
        s_txt = 1.0 / np.sqrt(TEXT_DIM)
        s_ff = 1.0 / np.sqrt(2 * IMAGE_DIM)
        return {'x': jax.random.normal(ks[0], (B, N, IMAGE_DIM), jnp.float32), 'y': jax.random.normal(ks[1], (B, M, TEXT_DIM), jnp.float32), 'Wq': jax.random.normal(ks[2], (IMAGE_DIM, IMAGE_DIM), jnp.float32) * s_img, 'bq': jax.random.normal(ks[3], (IMAGE_DIM,), jnp.float32) * s_img, 'Wk': jax.random.normal(ks[4], (TEXT_DIM, IMAGE_DIM), jnp.float32) * s_txt, 'bk': jax.random.normal(ks[5], (IMAGE_DIM,), jnp.float32) * s_txt, 'Wv': jax.random.normal(ks[6], (TEXT_DIM, IMAGE_DIM), jnp.float32) * s_txt, 'bv': jax.random.normal(ks[7], (IMAGE_DIM,), jnp.float32) * s_txt, 'W1': jax.random.normal(ks[8], (IMAGE_DIM, 2 * IMAGE_DIM), jnp.float32) * s_img, 'b1': jax.random.normal(ks[9], (2 * IMAGE_DIM,), jnp.float32) * s_img, 'W2': jax.random.normal(ks[10], (2 * IMAGE_DIM, IMAGE_DIM), jnp.float32) * s_ff, 'b2': jax.random.normal(ks[11], (IMAGE_DIM,), jnp.float32) * s_ff}
    _L1_xattn_all = _L1_xattn_setup()
    _L1_xattn_in = {k: v for k, v in _L1_xattn_all.items() if k in ('Wq', 'bq', 'Wk', 'bk', 'Wv', 'bv', 'W1', 'b1', 'W2', 'b2')}
    del _L1_xattn_all

    def _L1_ffn_setup():
        import jax, jax.numpy as jnp
        import numpy as np
        D_MODEL = 128
        D_FF = 512
        N_EXPERTS = 8
        TOP_K = 2
        B, L = (4, 256)
        key = jax.random.key(seed)
        ks = jax.random.split(key, 5)
        x = jax.random.normal(ks[0], (B, L, D_MODEL), dtype=jnp.float32)
        Wg = jax.random.normal(ks[1], (D_MODEL, N_EXPERTS), dtype=jnp.float32) * 0.02
        W1 = jax.random.normal(ks[2], (N_EXPERTS, D_MODEL, D_FF), dtype=jnp.float32) * 0.02
        W2 = jax.random.normal(ks[3], (N_EXPERTS, D_FF, D_MODEL), dtype=jnp.float32) * 0.02
        W3 = jax.random.normal(ks[4], (N_EXPERTS, D_MODEL, D_FF), dtype=jnp.float32) * 0.02
        return {'x': x, 'Wg': Wg, 'W1': W1, 'W2': W2, 'W3': W3}
    _L1_ffn_all = _L1_ffn_setup()
    _L1_ffn_in = {k: v for k, v in _L1_ffn_all.items() if k in ('Wg', 'W1', 'W2', 'W3')}
    del _L1_ffn_all
    return {'x': x, 'ctx_768': ctx_768, 'L0_xattn_Wq': _L0_xattn_in['Wq'], 'L0_xattn_Wk': _L0_xattn_in['Wk'], 'L0_xattn_Wv': _L0_xattn_in['Wv'], 'L0_xattn_Wo': _L0_xattn_in['Wo'], 'L0_xattn_bo': _L0_xattn_in['bo'], 'L0_ffn_w1': _L0_ffn_in['w1'], 'L0_ffn_b1': _L0_ffn_in['b1'], 'L0_ffn_w2': _L0_ffn_in['w2'], 'L0_ffn_b2': _L0_ffn_in['b2'], 'L1_xattn_Wq': _L1_xattn_in['Wq'], 'L1_xattn_bq': _L1_xattn_in['bq'], 'L1_xattn_Wk': _L1_xattn_in['Wk'], 'L1_xattn_bk': _L1_xattn_in['bk'], 'L1_xattn_Wv': _L1_xattn_in['Wv'], 'L1_xattn_bv': _L1_xattn_in['bv'], 'L1_xattn_W1': _L1_xattn_in['W1'], 'L1_xattn_b1': _L1_xattn_in['b1'], 'L1_xattn_W2': _L1_xattn_in['W2'], 'L1_xattn_b2': _L1_xattn_in['b2'], 'L1_ffn_Wg': _L1_ffn_in['Wg'], 'L1_ffn_W1': _L1_ffn_in['W1'], 'L1_ffn_W2': _L1_ffn_in['W2'], 'L1_ffn_W3': _L1_ffn_in['W3']}

def reference(x, ctx_768, L0_xattn_Wq, L0_xattn_Wk, L0_xattn_Wv, L0_xattn_Wo, L0_xattn_bo, L0_ffn_w1, L0_ffn_b1, L0_ffn_w2, L0_ffn_b2, L1_xattn_Wq, L1_xattn_bq, L1_xattn_Wk, L1_xattn_bk, L1_xattn_Wv, L1_xattn_bv, L1_xattn_W1, L1_xattn_b1, L1_xattn_W2, L1_xattn_b2, L1_ffn_Wg, L1_ffn_W1, L1_ffn_W2, L1_ffn_W3):
    import jax
    import jax.numpy as jnp

    def _L0_xattn_ref(x, context, Wq, Wk, Wv, Wo, bo):
        import jax, jax.numpy as jnp
        import numpy as np
        QUERY_DIM = 128
        CONTEXT_DIM = 96
        HEADS = 8
        DIM_HEAD = 64
        INNER = HEADS * DIM_HEAD
        B, S, _ = x.shape
        L = context.shape[1]
        scale = DIM_HEAD ** (-0.5)
        q = (x @ Wq).reshape(B, S, HEADS, DIM_HEAD).transpose(0, 2, 1, 3)
        k = (context @ Wk).reshape(B, L, HEADS, DIM_HEAD).transpose(0, 2, 1, 3)
        v = (context @ Wv).reshape(B, L, HEADS, DIM_HEAD).transpose(0, 2, 1, 3)
        attn = jnp.einsum('bhsd,bhld->bhsl', q, k) * scale
        attn = jax.nn.softmax(attn, axis=-1)
        out = jnp.einsum('bhsl,bhld->bhsd', attn, v)
        out = out.transpose(0, 2, 1, 3).reshape(B, S, INNER)
        return out @ Wo + bo

    def _L0_ffn_ref(x, w1, b1, w2, b2):
        import jax, jax.numpy as jnp
        import numpy as np
        MANT_BITS = 8
        _PWL_X = jnp.linspace(-4.0, 4.0, 33, dtype=jnp.float32)
        _PWL_Y = 0.5 * _PWL_X * (1.0 + jax.lax.erf(_PWL_X / jnp.sqrt(jnp.float32(2.0))))

        def float2fix(x, mantissa_bits):
            s = jnp.float32(2.0 ** mantissa_bits)
            q = jnp.round(x * s) / s
            return x + jax.lax.stop_gradient(q - x)

        def pwlin_gelu_basic(x, mantissa_bits_in, mantissa_bits_out):
            xq = float2fix(x, mantissa_bits_in)
            y = jnp.interp(xq, _PWL_X, _PWL_Y)
            y = jnp.where(xq > 4.0, xq, jnp.where(xq < -4.0, jnp.float32(0.0), y))
            return float2fix(y, mantissa_bits_out)
        h = jnp.einsum('bsd,df->bsf', x, w1) + b1
        h = float2fix(h, MANT_BITS)
        h = pwlin_gelu_basic(h, MANT_BITS, MANT_BITS)
        h = float2fix(h, MANT_BITS)
        out = jnp.einsum('bsf,fd->bsd', h, w2) + b2
        return float2fix(out, MANT_BITS)

    def _L1_xattn_ref(x, y, Wq, bq, Wk, bk, Wv, bv, W1, b1, W2, b2):
        import jax, jax.numpy as jnp
        import numpy as np
        IMAGE_DIM = 128
        TEXT_DIM = 96
        NUM_HEADS = 16
        HEAD_DIM = IMAGE_DIM // NUM_HEADS
        B, N, _ = x.shape
        M = y.shape[1]
        q = (x @ Wq + bq).reshape(B, N, NUM_HEADS, HEAD_DIM)
        k = (y @ Wk + bk).reshape(B, M, NUM_HEADS, HEAD_DIM)
        v = (y @ Wv + bv).reshape(B, M, NUM_HEADS, HEAD_DIM)
        scale = 1.0 / np.sqrt(HEAD_DIM)
        scores = jnp.einsum('bnhd,bmhd->bhnm', q, k) * scale
        attn = jax.nn.softmax(scores, axis=-1)
        out = jnp.einsum('bhnm,bmhd->bnhd', attn, v).reshape(B, N, IMAGE_DIM)
        h = jax.nn.relu(out @ W1 + b1)
        return h @ W2 + b2

    def _L1_ffn_ref(x, Wg, W1, W2, W3):
        import jax, jax.numpy as jnp
        import numpy as np
        D_MODEL = 128
        D_FF = 512
        N_EXPERTS = 8
        TOP_K = 2
        B, L = (4, 256)
        Bb, Ll, D = x.shape
        t = x.reshape(-1, D)
        T = t.shape[0]
        E = Wg.shape[1]
        logits = t @ Wg
        probs = jax.nn.softmax(logits, axis=-1)
        top_v, top_i = jax.lax.top_k(probs, TOP_K)
        top_v = top_v / (jnp.sum(top_v, axis=-1, keepdims=True) + 1e-08)
        comb = jnp.zeros((T, E), dtype=t.dtype).at[jnp.arange(T)[:, None], top_i].add(top_v)
        out = jnp.zeros_like(t)
        for e in range(E):
            h = jax.nn.silu(t @ W1[e]) * (t @ W3[e])
            out = out + comb[:, e:e + 1] * (h @ W2[e])
        return out.reshape(Bb, Ll, D)
    x = x + _L0_xattn_ref(_layernorm(x, axis=-1), ctx_768, L0_xattn_Wq, L0_xattn_Wk, L0_xattn_Wv, L0_xattn_Wo, L0_xattn_bo)
    x = x + _L0_ffn_ref(_layernorm(x, axis=-1), L0_ffn_w1, L0_ffn_b1, L0_ffn_w2, L0_ffn_b2)
    x = x + _L1_xattn_ref(_layernorm(x, axis=-1), ctx_768, L1_xattn_Wq, L1_xattn_bq, L1_xattn_Wk, L1_xattn_bk, L1_xattn_Wv, L1_xattn_bv, L1_xattn_W1, L1_xattn_b1, L1_xattn_W2, L1_xattn_b2)
    x = x + _L1_ffn_ref(_layernorm(x, axis=-1), L1_ffn_Wg, L1_ffn_W1, L1_ffn_W2, L1_ffn_W3)
    return x

_drawn_inputs = setup_inputs


def setup_inputs(seed=0):
    import zlib

    import numpy as np

    out = dict(_drawn_inputs(seed))
    spreads = {}
    factors = {'L0_xattn_bo': 6.15,
     'L0_ffn_b1': 3.888,
     'L1_xattn_bq': 4.775,
     'L1_xattn_bk': 8.0,
     'L1_ffn_Wg': 8.0,
     'L1_ffn_W1': 8.0,
     'L1_ffn_W2': 8.0,
     'L1_ffn_W3': 8.0}
    for name, (base, spread) in spreads.items():
        noise = np.random.default_rng([zlib.crc32(name.encode()), seed]).standard_normal(out[name].shape)
        drawn = base * np.exp(spread * noise) if base else spread * noise
        out[name] = jnp.asarray(drawn.astype(out[name].dtype))
    for name, factor in factors.items():
        out[name] = (out[name] * factor).astype(out[name].dtype)
    return out
```

```python
from contextlib import ExitStack

import concourse.bass as bass
from concourse import mybir

ALU = mybir.AluOpType
ACT = mybir.ActivationFunctionType
F32 = mybir.dt.float32
F16 = mybir.dt.float16
AX_X = mybir.AxisListType.X

P = 128
B = 4
S = 256
T = 2
C = 512
CD = 96
KT = C // P
H0, DH0 = 8, 64
H1, DH1 = 16, 8
M0 = H0 * DH0 // P
FF = 4
E = 8
MAGIC = 12582912.0
FIX = 256.0
EPS = 1e-5
SEL0 = 64
SEL1 = 96
VW = DH1 + 1


def build(nc, t, out):
    ctx = ExitStack()
    with ctx:
        def sb(name, shape, dt=F32):
            return ctx.enter_context(nc.sbuf_tensor(name, shape, dt))

        def sem(name):
            return ctx.enter_context(nc.semaphore(name))

        def sems(name, n):
            return [sem(f"{name}{i}") for i in range(n)]

        ident = sb("ident", [P, P])
        x_sb = sb("x_sb", [P, B * T, P])
        cT = sb("cT", [CD, B * C])
        wq0 = sb("wq0", [P, H0 * DH0])
        wk0 = sb("wk0", [CD, H0 * DH0])
        wv0 = sb("wv0", [CD, H0 * DH0])
        wo0 = sb("wo0", [P, M0, P])
        f0w1 = sb("f0w1", [P, FF * P])
        f0w2 = sb("f0w2", [P, FF, P])
        f0b1 = sb("f0b1", [P, FF])
        wq1 = sb("wq1", [P, P])
        wk1 = sb("wk1", [CD, P])
        wv1 = sb("wv1", [CD, P])
        bq1 = sb("bq1", [P, 1])
        bk1 = sb("bk1", [P, 1])
        f1w1 = sb("f1w1", [P, 2 * P])
        f1w2 = sb("f1w2", [P, 2, P])
        f1b1 = sb("f1b1", [P, 2])
        wg = sb("wg", [P, E])
        bo0 = sb("bo0", [P, P])
        f0b2 = sb("f0b2", [P, P])
        bv1 = sb("bv1", [P, P])
        f1b2 = sb("f1b2", [P, P])
        region = sb("region", [P, 24576], F16)
        kA = region[:, 0:8192].rearrange("p (b h k) -> p b h k", b=2, h=H0)
        kB = region[:, 8192:16384].rearrange("p (b h k) -> p b h k", b=2, h=H0)
        qA = region[:, 16384:20480].rearrange("p (b h k) -> p b h k", b=2, h=H0)
        qB = region[:, 20480:24576].rearrange("p (b h k) -> p b h k", b=2, h=H0)
        ew = [region[:, 8192 * i:8192 * (i + 1)].rearrange("p (s e n) -> p s e n", s=2, e=E) for i in range(3)]
        kS = sb("kS", [P, 2, H1, C], F16)
        qS = sb("qS", [P, 2, H1, S], F16)
        kx = sb("kx", [P, 2, M0, C], F16)
        qx = sb("qx", [P, 2, M0, S], F16)
        v0 = sb("v0", [P, 2, KT, H0 * DH0])
        VR = VW * H1 + 32 - VW
        v1 = v0[:, 1, :, :].rearrange("p k n -> p (k n)")[:, 0:2 * KT * VR].rearrange("p (b k n) -> p b k n", b=2, k=KT)
        stage = v0[:, 0, 0:2, :]
        probs = sb("probs", [P, 8, KT * S])
        raw = probs[:, 0:2, :].rearrange("p a b -> p (a b)")[:, 0:B * KT * CD].rearrange("p (c d) -> p c d", d=CD)
        xn = sb("xn", [P, 2, T, P])
        xT = sb("xT", [P, 2, S])
        xh = qS[:, 0, 0:8, :].rearrange("p h n -> p (h n)").rearrange("p (s n) -> p s n", s=2)
        cmp_ = kS[:, 0, 0:4, :].rearrange("p h n -> p (h n)").bitcast(F32).rearrange("p (s t e f) -> p s t e f", s=2, t=B * T, e=E)
        mx = sb("mx", [P, 2, T, H1])
        stats = sb("stats", [P, T, 6])
        meanvar = sb("meanvar", [P, 2, T, 2])
        veps = sb("veps", [P, 2, T])
        rstd = sb("rstd", [P, 2, T])
        mhalf = sb("mhalf", [P, T])
        ones = sb("ones", [P, 32])
        quarter = sb("quarter", [P, 1])
        osb = sb("osb", [P, 4, S])
        ssb = sb("ssb", [P, 2, S])
        rden = sb("rden", [P, T, H1])
        a0 = sb("a0", [P, T, M0 * P])
        aT = sb("aT", [P, T, M0, P])
        ytmp = sb("ytmp", [P, T, P])
        ztmp = sb("ztmp", [P, T, P])
        lg = kS[:, 0, 4:6, :].rearrange("p h n -> p (h n)").bitcast(F32).rearrange("p (i t e) -> p i t e", i=8, t=B * T)
        gs = sb("gs", [P, 4, B * T])
        tri = sb("tri", [P, E, E])
        comb = sb("comb", [P, B * T, E])
        sg = probs[:, 0, :].rearrange("p (a b) -> p a b", a=2)
        hp = probs[:, 1, :].rearrange("p (a b) -> p a b", a=2)
        hh = probs[:, 2:6, :].bitcast(F16).rearrange("p (b s) (f n) -> p b s f n", b=2, f=FF)

        p_max = ctx.enter_context(nc.psum_tensor("p_max", [P, 2, 512], F32))
        p_sc = ctx.enter_context(nc.psum_tensor("p_sc", [P, 2, 512], F32))
        p_o = ctx.enter_context(nc.psum_tensor("p_o", [P, 2, 512], F32))
        p_misc = ctx.enter_context(nc.psum_tensor("p_misc", [P, 2, 512], F32))

        dk = nc.dram_tensor("k_scratch", (B, P, 2, C), F16).ap()
        dq = nc.dram_tensor("q_scratch", (B, P, 2, S), F16).ap()

        ld_x, ld_c, ld_w0, ld_w1, ld_w2 = (sem(f"ld_{n}") for n in ("x", "c", "w0", "w1", "w2"))
        ld_stage = sems("ld_stage", 2)
        stage_free = sem("stage_free")
        consts = sem("consts")
        misc_full = sems("misc_full", 2)
        misc_free = sems("misc_free", 2)
        ln_var, ln_rstd, ln_xn = sem("ln_var"), sem("ln_rstd"), sem("ln_xn")
        k_hi, q_hi = sem("k_hi"), sem("q_hi")
        k_stacked, q_stacked = sem("k_stacked"), sem("q_stacked")
        k_bounced, q_bounced = sem("k_bounced"), sem("q_bounced")
        max_full, max_free = sems("max_full", 2), sems("max_free", 2)
        sc_full, sc_free = sems("sc_full", 2), sems("sc_free", 2)
        av_done, o_free = sem("av_done"), sem("o_free")
        nodes = sem("nodes")
        pwl_j = sem("pwl_j")
        pwl_out = sem("pwl_out")
        h1_relu = sem("h1_relu")
        gate_d, gate_e, xh_hi = sem("gate_d"), sem("gate_e"), sem("xh_hi")
        gu_full, sg_done, hp_done, hh_done, hl_done = (sem(n) for n in ("gu_full", "sg_done", "hp_done", "hh_done", "hl_done"))
        y_full, y_free = sem("y_full"), sem("y_free")
        dve_chain, act_chain, pool_chain = sem("dve_chain"), sem("act_chain"), sem("pool_chain")
        stored = sem("stored")

        misc = {}

        def misc_take(pe, key):
            n = len(misc)
            bank, use = n % 2, n // 2 + 1
            if use > 1:
                pe.wait_ge(misc_free[bank], use - 1)
            misc[key] = (bank, use)
            return p_misc[:, bank, :], misc_full[bank]

        def misc_wait(eng, key):
            bank, use = misc[key]
            eng.wait_ge(misc_full[bank], use)
            return p_misc[:, bank, :], misc_free[bank]

        def misc_done(eng, key):
            bank, use = misc[key]
            eng.wait_ge(misc_free[bank], use)

        block = ctx.enter_context(nc.Block())

        @block.tensor
        def _(pe):
            def transposes(key, parts, ready=()):
                for s, v in ready:
                    pe.wait_ge(s, v)
                ps, full = misc_take(pe, key)
                at = 0
                for src in parts:
                    k, m = src.shape
                    last = pe.transpose(ps[0:m, at:at + k], src, ident[0:k, 0:k])
                    at += k
                last.then_inc(full, 1)

            def context(b):
                transposes(("cT", b), [raw[:, b * KT + i, :] for i in range(KT)])

            def keys0(b):
                misc_done(pe, ("cT", b))
                for m in range(M0):
                    ps, full = misc_take(pe, ("k0", b, m))
                    pe.matmul(ps, wk0[:, m * P:(m + 1) * P], cT[:, b * C:(b + 1) * C], start=True, stop=True).then_inc(full, 1)

            def values0(b):
                for kt in range(KT):
                    ps, full = misc_take(pe, ("v0", b, kt))
                    pe.matmul(ps, cT[:, b * C + kt * P:b * C + (kt + 1) * P], wv0[:, :], start=True, stop=True).then_inc(full, 1)

            def xt(n):
                transposes(("xT", n), [xn[:, n % 2, i, :] for i in range(T)], [(ln_xn, n + 1)])

            def queries0(b):
                xt(b)
                misc_done(pe, ("xT", b))
                for i in range(2):
                    ps, full = misc_take(pe, ("q0", b, i))
                    for m in (2 * i, 2 * i + 1):
                        last = pe.matmul(ps[:, (m % 2) * S:(m % 2 + 1) * S], wq0[:, m * P:(m + 1) * P], xT[:, b % 2, :],
                                         start=True, stop=True)
                    last.then_inc(full, 1)

            def maxima(u, q, k):
                for i in range(T):
                    if u:
                        pe.wait_ge(max_free[i], u)
                    pe.matmul(p_max[:, i, :], q[:, i * P:(i + 1) * P], k, start=True, stop=True).then_inc(max_full[i], 1)

            def max_rows(key, u, b, h):
                transposes(key, [mx[:, b % 2, i, 0:h] for i in range(T)], [(max_free[0], u), (max_free[1], u)])

            def scores(u, pairs):
                for half in range(2):
                    if u:
                        pe.wait_ge(sc_free[half], u)
                    for j in range(2):
                        kt = 2 * half + j
                        for i, (k, q) in enumerate(pairs):
                            last = pe.matmul(p_sc[:, half, j * S:(j + 1) * S], k[:, kt * P:(kt + 1) * P], q,
                                             start=(i == 0), stop=(i == len(pairs) - 1))
                    last.then_inc(sc_full[half], 1)

            def attend(u, prev):
                pe.wait_ge(sc_free[0], u)
                pe.wait_ge(sc_free[1], u)
                if prev:
                    pe.wait_ge(o_free, prev)

            def attend0(b, g):
                n = b * 2 + g
                attend(4 * (n + 1), n)
                for m in range(2):
                    for kt in range(KT):
                        for i in range(2):
                            h = 4 * g + 2 * m + i
                            pe.matmul(p_o[64 * i:64 * i + 64, 0, m * S:(m + 1) * S], v0[:, b % 2, kt, h * DH0:(h + 1) * DH0],
                                      probs[:, h % 8, kt * S:(kt + 1) * S], start=(kt == 0), stop=(kt == KT - 1))
                for kt in range(KT):
                    for j in range(4):
                        last = pe.matmul(p_o[32 * j:32 * j + 32, 1, 0:S], ones[:, :],
                                         probs[:, (4 * g + j) % 8, kt * S:(kt + 1) * S], start=(kt == 0), stop=(kt == KT - 1),
                                         tile_position=(0, 32 * j))
                last.then_inc(av_done, 1)

            def attend1(b, g):
                n = B * 2 + b * 4 + g
                u = B * H0 + b * H1 + 4 * (g + 1)
                attend(u, n - 1 if n > B * 2 else n)
                for kt in range(KT):
                    for j in range(4):
                        h = 4 * g + j
                        last = pe.matmul(p_o[32 * j:32 * j + 32, n % 2, 0:S], v1[:, b % 2, kt, h * VW:h * VW + 32],
                                         probs[:, h % 8, kt * S:(kt + 1) * S], start=(kt == 0), stop=(kt == KT - 1),
                                         tile_position=(0, 32 * j))
                last.then_inc(av_done, 1)

            def project0(b):
                pe.wait_ge(o_free, 2 * (b + 1))
                for i in range(T):
                    transposes(("sT", b, i), [ssb[:, g, i * P:(i + 1) * P] for g in range(2)])
                    transposes(("oT", b, i), [osb[:, m, i * P:(i + 1) * P] for m in range(M0)])
                for i in range(T):
                    misc_done(pe, ("oT", b, i))
                    transposes(("aT", b, i), [a0[:, i, m * P:(m + 1) * P] for m in range(M0)])
                for i in range(T):
                    misc_done(pe, ("aT", b, i))
                    ps, full = misc_take(pe, ("y0", b, i))
                    for m in range(M0):
                        last = pe.matmul(ps[:, 0:P], aT[:, i, m, :], wo0[:, m, :], start=(m == 0), stop=(m == M0 - 1))
                    last.then_inc(full, 1)

            def max0(b, h):
                if h == 0:
                    pe.wait_ge(k_stacked, 96 * (b + 1))
                    pe.wait_ge(q_stacked, 96 * (b + 1))
                maxima(b * H0 + h, qA[:, b % 2, h, :], kA[:, b % 2, h, :])

            def front0(b):
                keys0(b)
                values0(b)
                queries0(b)

            pe.wait_ge(ld_c, 16)
            pe.wait_ge(consts, 1)
            for b in range(B):
                context(b)
            pe.wait_ge(ld_w0, 48)
            front0(0)
            pe.wait_ge(ld_w1, 16 * 6)
            for h in range(H0):
                max0(0, h)
            pe.wait_ge(consts, 2)
            max_rows(("mT0", 0), H0, 0, H0)
            for b in range(B):
                if b + 1 < B:
                    front0(b + 1)
                misc_done(pe, ("mT0", b))
                for h in range(H0):
                    scores(b * H0 + h, [(kA[:, b % 2, h, :], qA[:, b % 2, h, :]), (kB[:, b % 2, h, :], qB[:, b % 2, h, :])])
                    if h == 5:
                        attend0(b, 0)
                    if b + 1 < B and h >= 2:
                        max0(b + 1, h - 2)
                if b + 1 < B:
                    max0(b + 1, 6)
                    max0(b + 1, 7)
                attend0(b, 1)
                if b + 1 < B:
                    max_rows(("mT0", b + 1), (b + 2) * H0, b + 1, H0)
                project0(b)

            def up0(b):
                xt(B + b)
                misc_done(pe, ("xT", B + b))
                for i in range(2):
                    ps, full = misc_take(pe, ("h0", b, i))
                    for f in (2 * i, 2 * i + 1):
                        last = pe.matmul(ps[:, (f % 2) * S:(f % 2 + 1) * S], f0w1[:, f * P:(f + 1) * P], xT[:, (B + b) % 2, :],
                                         start=True, stop=True)
                    last.then_inc(full, 1)

            def down0(b):
                pe.wait_ge(pwl_out, b + 1)
                ps, full = misc_take(pe, ("z0", b))
                for i in range(T):
                    for f in range(FF):
                        last = pe.matmul(ps[:, i * P:(i + 1) * P], probs[:, 7, f * S + i * P:f * S + (i + 1) * P], f0w2[:, f, :],
                                         start=(f == 0), stop=(f == FF - 1))
                last.then_inc(full, 1)

            for b in range(B):
                up0(b)
                down0(b)

            def front1(b):
                ps, full = misc_take(pe, ("k1", b))
                pe.matmul(ps, wk1[:, :], cT[:, b * C:(b + 1) * C], start=True, stop=True).then_inc(full, 1)
                ps, full = misc_take(pe, ("v1", b))
                for kt in range(KT):
                    last = pe.matmul(ps[:, kt * P:(kt + 1) * P], cT[:, b * C + kt * P:b * C + (kt + 1) * P], wv1[:, :],
                                     start=True, stop=True)
                last.then_inc(full, 1)
                xt(2 * B + b)
                misc_done(pe, ("xT", 2 * B + b))
                ps, full = misc_take(pe, ("q1", b))
                pe.matmul(ps[:, 0:S], wq1[:, :], xT[:, b % 2, :], start=True, stop=True).then_inc(full, 1)

            def max1(b, h):
                if h == 0:
                    pe.wait_ge(k_stacked, 96 * B + 48 * (b + 1))
                    pe.wait_ge(q_stacked, 96 * B + 48 * (b + 1))
                maxima(B * H0 + b * H1 + h, qS[0:SEL1, b % 2, h, :], kS[0:SEL1, b % 2, h, :])

            def project1(b):
                pe.wait_ge(o_free, 2 * B + 4 * (b + 1))
                for i in range(T):
                    transposes(("oT1", b, i), [osb[:, g, i * P:(i + 1) * P] for g in range(4)])
                misc_done(pe, ("oT1", b, 0))
                misc_done(pe, ("oT1", b, 1))
                transposes(("aT1", b), [a0[:, i, 0:P] for i in range(T)])
                misc_done(pe, ("aT1", b))
                ps, full = misc_take(pe, ("h1", b))
                for f in range(2):
                    last = pe.matmul(ps[:, f * S:(f + 1) * S], f1w1[:, f * P:(f + 1) * P],
                                     aT[:, 0, 0:2, :].rearrange("p a b -> p (a b)"), start=True, stop=True)
                last.then_inc(full, 1)
                misc_done(pe, ("h1", b))
                ps, full = misc_take(pe, ("y1", b))
                for i in range(T):
                    for f in range(2):
                        last = pe.matmul(ps[:, i * P:(i + 1) * P], ssb[:, f, i * P:(i + 1) * P], f1w2[:, f, :],
                                         start=(f == 0), stop=(f == 1))
                last.then_inc(full, 1)

            pe.wait_ge(ld_w2, 16 * 12)
            front1(0)
            for h in range(H1):
                max1(0, h)
            max_rows(("mT1", 0), B * H0 + H1, 0, H1)
            for b in range(B):
                if b + 1 < B:
                    front1(b + 1)
                misc_done(pe, ("mT1", b))
                for h in range(H1):
                    scores(B * H0 + b * H1 + h, [(kS[:, b % 2, h, :], qS[:, b % 2, h, :])])
                    if h % 4 == 1 and h > 4:
                        attend1(b, h // 4 - 1)
                    if b + 1 < B and h >= 2:
                        max1(b + 1, h - 2)
                if b + 1 < B:
                    max1(b + 1, H1 - 2)
                    max1(b + 1, H1 - 1)
                attend1(b, 3)
                if b + 1 < B:
                    max_rows(("mT1", b + 1), B * H0 + (b + 2) * H1, b + 1, H1)
                project1(b)

            for b in range(B):
                xt(3 * B + b)
            for b in range(B):
                misc_done(pe, ("xT", 3 * B + b))
                ps, full = misc_take(pe, ("lg", b))
                for i in range(T):
                    last = pe.matmul(ps[:, i * E:(i + 1) * E], osb[:, b, i * P:(i + 1) * P], wg[:, :], start=True, stop=True)
                last.then_inc(full, 1)

            def gate_up(n, f):
                e, half = n // 2, n % 2
                k = n * FF + f
                if k >= 2:
                    pe.wait_ge(hp_done, k - 1)
                for ps, w in ((p_max, ew[0]), (p_sc, ew[1])):
                    for i, (ws, xs) in enumerate(((0, 0), (0, 1), (1, 0))):
                        last = pe.matmul(ps[:, f % 2, :], w[:, ws, e, f * P:(f + 1) * P], xh[:, xs, half * C:(half + 1) * C],
                                         start=(i == 0), stop=(i == 2))
                last.then_inc(gu_full, 1)

            def down(n):
                pe.wait_ge(hl_done, FF * (n + 1))
                if n >= 2:
                    pe.wait_ge(y_free, n - 1)
                e = n // 2
                for i in range(4):
                    at = 0
                    for f in range(FF):
                        for hs, ws in ((0, 0), (0, 1), (1, 0)):
                            last = pe.matmul(p_o[:, n % 2, i * P:(i + 1) * P], hh[:, n % 2, hs, f, i * P:(i + 1) * P],
                                             ew[2][:, ws, e, f * P:(f + 1) * P], start=(at == 0), stop=(at == 3 * FF - 1))
                            at += 1
                last.then_inc(y_full, 1)

            pe.wait_ge(stage_free, 24)
            for n in range(2 * E):
                for f in range(FF):
                    gate_up(n, f)
                    if f == 1 and n:
                        down(n - 1)
            down(2 * E - 1)

        @block.vector
        def _(dve):
            chain = [0]

            def link(ins):
                chain[0] += 1
                ins.then_inc(dve_chain, 1)
                dve.wait_ge(dve_chain, chain[0])

            def norm(n, b):
                for i in range(T):
                    last = dve.bn_stats(stats[:, i, :], x_sb[:, b * T + i, :])
                link(last)
                for i in range(T):
                    last = dve.bn_aggr(meanvar[:, n % 2, i, :], stats[:, i, :])
                last.then_inc(ln_var, 1)
                dve.wait_ge(ln_rstd, n + 1)
                for i in range(T):
                    last = dve.tensor_scalar(xn[:, n % 2, i, :], x_sb[:, b * T + i, :], meanvar[:, n % 2, i, 0:1],
                                             rstd[:, n % 2, i:i + 1], ALU.subtract, ALU.mult)
                last.then_inc(ln_xn, 1)

            def keys_low0(b):
                for m in range(M0):
                    dve.wait_ge(k_hi, b * M0 + m + 1)
                    ps, free = misc_wait(dve, ("k0", b, m))
                    dve.tensor_tensor(kx[:, 1, m, :], ps, kx[:, 0, m, :], ALU.subtract).then_inc(free, 1)

            def queries_low0(b):
                for i in range(2):
                    dve.wait_ge(q_hi, b * 2 + i + 1)
                    ps, free = misc_wait(dve, ("q0", b, i))
                    dve.tensor_tensor(qx[:, 1, 2 * i:2 * i + 2, :].rearrange("p m n -> p (m n)"), ps,
                                      qx[:, 0, 2 * i:2 * i + 2, :].rearrange("p m n -> p (m n)"), ALU.subtract).then_inc(free, 1)

            def maxima(u, b, h):
                for i in range(T):
                    dve.wait_ge(max_full[i], u + 1)
                    dve.tensor_reduce(mx[:, b % 2, i, h:h + 1], p_max[:, i, :], AX_X, ALU.max).then_inc(max_free[i], 1)

            def max_rows(key, dst, h):
                ps, free = misc_wait(dve, key)
                src = ps[0:h, 0:S].unsqueeze(1).broadcast_to([h, h, S])
                dve.tensor_copy(dst, src).then_inc(free, 1)

            def front0(b):
                if b == 0:
                    dve.wait_ge(ld_x, 16)
                norm(b, b)
                keys_low0(b)
                queries_low0(b)

            def add_to_x(b, i, key, bias, at=0, last_of=True):
                ps, free = misc_wait(dve, key)
                ins = dve.tensor_tensor(ytmp[:, i, :], ps[:, at:at + P], bias, ALU.add)
                if last_of:
                    ins.then_inc(free, 1)
                    misc_done(dve, key)
                else:
                    link(ins)
                link(dve.tensor_tensor(x_sb[:, b * T + i, :], x_sb[:, b * T + i, :], ytmp[:, i, :], ALU.add))

            def project0(b):
                for i in range(T):
                    ps, free = misc_wait(dve, ("sT", b, i))
                    dve.reciprocal(rden[:, i, 0:H0], ps[:, 0:2 * P].rearrange("p (h r) -> p h r", r=32)[:, :, 0]).then_inc(free, 1)
                    misc_done(dve, ("sT", b, i))
                    ps, free = misc_wait(dve, ("oT", b, i))
                    dve.tensor_tensor(a0[:, i, :].rearrange("p (h d) -> p h d", h=H0), ps.rearrange("p (h d) -> p h d", h=H0),
                                      rden[:, i, 0:H0].unsqueeze(2).broadcast_to([P, H0, DH0]), ALU.mult).then_inc(free, 1)
                for i in range(T):
                    add_to_x(b, i, ("y0", b, i), bo0[:, :])

            front0(0)
            for h in range(H0):
                maxima(h, 0, h)
            max_rows(("mT0", 0), qB[SEL0:SEL0 + H0, 0, :, :], H0)
            dve.wait_ge(ld_w1, 16 * 6)
            for b in range(B):
                if b + 1 < B:
                    front0(b + 1)
                    for h in range(H0):
                        maxima((b + 1) * H0 + h, b + 1, h)
                    max_rows(("mT0", b + 1), qB[SEL0:SEL0 + H0, (b + 1) % 2, :, :], H0)
                project0(b)

            def interpolate(b):
                A, N, Cl, J, Y0, Y1, F, O = (probs[:, i, :] for i in range(8))
                for i in range(2):
                    ps, free = misc_wait(dve, ("h0", b, i))
                    for f in (2 * i, 2 * i + 1):
                        last = dve.tensor_scalar(A[:, f * S:(f + 1) * S], ps[:, (f % 2) * S:(f % 2 + 1) * S],
                                                 f0b1[:, f:f + 1], FIX, ALU.add, ALU.mult)
                    last.then_inc(free, 1)
                    misc_done(dve, ("h0", b, i))
                link(dve.tensor_scalar(N, A, MAGIC, MAGIC, ALU.add, ALU.subtract))
                link(dve.tensor_scalar(Cl, N, -4 * FIX, 4 * FIX - 1, ALU.max, ALU.min))
                link(dve.tensor_scalar(F, Cl, 1.0 / 64, -31.5 / 64, ALU.mult, ALU.add))
                dve.tensor_scalar(J, F, MAGIC, MAGIC, ALU.add, ALU.subtract).then_inc(pwl_j, 1)
                dve.wait_ge(pwl_j, b + 1)
                link(dve.scalar_tensor_tensor(F, J, -64.0, Cl, ALU.mult, ALU.add))
                dve.wait_ge(nodes, 2 * (b + 1))
                link(dve.tensor_tensor(Y1, Y1, Y0, ALU.subtract))
                link(dve.scalar_tensor_tensor(F, F, 4.0, Y1, ALU.mult, ALU.mult))
                link(dve.scalar_tensor_tensor(Y0, Y0, FIX, F, ALU.mult, ALU.add))
                link(dve.tensor_scalar(Y0, Y0, MAGIC, MAGIC + 4 * FIX - 1, ALU.add, ALU.subtract))
                dve.scalar_tensor_tensor(O, N, 4 * FIX - 1, Y0, ALU.max, ALU.add).then_inc(pwl_out, 1)
                dve.wait_ge(pwl_out, b + 1)

            def down0(b):
                ps, free = misc_wait(dve, ("z0", b))
                flat = ytmp[:, :, :].rearrange("p a b -> p (a b)")
                flat2 = ztmp[:, :, :].rearrange("p a b -> p (a b)")
                dve.scalar_tensor_tensor(ytmp[:, :, :], ps[:, 0:T * P].rearrange("p (a b) -> p a b", a=T), 1.0 / FIX,
                                         f0b2[:, :].unsqueeze(1).broadcast_to([P, T, P]), ALU.mult, ALU.add).then_inc(free, 1)
                misc_done(dve, ("z0", b))
                link(dve.tensor_scalar(flat2, flat, FIX, MAGIC, ALU.mult, ALU.add))
                link(dve.tensor_scalar(flat, flat2, MAGIC, 1.0 / FIX, ALU.subtract, ALU.mult))
                link(dve.tensor_tensor(x_sb[:, b * T:(b + 1) * T, :], x_sb[:, b * T:(b + 1) * T, :], ytmp[:, :, :], ALU.add))

            for b in range(B):
                norm(B + b, b)
                interpolate(b)
                down0(b)

            dve.wait_ge(ld_w2, 16 * 12)

            def front1(b):
                norm(2 * B + b, b)
                dve.wait_ge(k_hi, B * M0 + b + 1)
                ps, free = misc_wait(dve, ("k1", b))
                dve.scalar_tensor_tensor(kx[:, 1, 0, :], ps, bk1[:, 0:1], kx[:, 0, 0, :], ALU.add, ALU.subtract).then_inc(free, 1)
                ps, free = misc_wait(dve, ("v1", b))
                for kt in range(KT):
                    last = dve.tensor_tensor(v1[:, b % 2, kt, 0:VW * H1].rearrange("p (h c) -> p h c", c=VW)[:, :, 0:DH1],
                                             ps[:, kt * P:(kt + 1) * P].rearrange("p (h d) -> p h d", h=H1),
                                             bv1[:, :].rearrange("p (h d) -> p h d", h=H1), ALU.add)
                last.then_inc(free, 1)
                dve.wait_ge(q_hi, 2 * B + b + 1)
                ps, free = misc_wait(dve, ("q1", b))
                dve.scalar_tensor_tensor(qx[:, 1, 0, :], ps[:, 0:S], bq1[:, 0:1], qx[:, 0, 0, :], ALU.add, ALU.subtract).then_inc(free, 1)

            def project1(b):
                for i in range(T):
                    ps, free = misc_wait(dve, ("oT1", b, i))
                    cols = ps.rearrange("p (h r) -> p h r", r=32)
                    link(dve.reciprocal(rden[:, i, :], cols[:, :, DH1]))
                    dve.tensor_tensor(a0[:, i, 0:P].rearrange("p (h d) -> p h d", h=H1), cols[:, :, 0:DH1],
                                      rden[:, i, :].unsqueeze(2).broadcast_to([P, H1, DH1]), ALU.mult).then_inc(free, 1)
                for i in range(T):
                    add_to_x(b, i, ("y1", b), f1b2[:, :], at=i * P, last_of=(i == T - 1))

            front1(0)
            for h in range(H1):
                maxima(B * H0 + h, 0, h)
            max_rows(("mT1", 0), qS[SEL1:SEL1 + H1, 0, :, :], H1)
            for b in range(B):
                if b + 1 < B:
                    front1(b + 1)
                    for h in range(H1):
                        maxima(B * H0 + (b + 1) * H1 + h, b + 1, h)
                    max_rows(("mT1", b + 1), qS[SEL1:SEL1 + H1, (b + 1) % 2, :, :], H1)
                project1(b)

            for b in range(B):
                norm(3 * B + b, b)
                dve.wait_ge(xh_hi, b + 1)
                ps, free = misc_wait(dve, ("xT", 3 * B + b))
                dve.tensor_tensor(xh[:, 1, b * S:(b + 1) * S], ps[:, 0:S], xh[:, 0, b * S:(b + 1) * S], ALU.subtract).then_inc(free, 1)
            NT = B * T
            logit, dif, ex, prob, picked = (lg[:, i, :, :] for i in range(5))

            def wide(v):
                return v.unsqueeze(2).broadcast_to([P, NT, E])

            for b in range(B):
                ps, free = misc_wait(dve, ("lg", b))
                last = dve.tensor_copy(logit[:, b * T:(b + 1) * T, :], ps[:, 0:T * E].rearrange("p (t e) -> p t e", t=T))
                last.then_inc(free, 1)
                misc_done(dve, ("lg", b))
            link(dve.tensor_reduce(gs[:, 0, :], logit, AX_X, ALU.max))
            dve.tensor_tensor(dif, logit, wide(gs[:, 0, :]), ALU.subtract).then_inc(gate_d, 1)
            dve.wait_ge(gate_e, 1)
            link(dve.tensor_reduce(gs[:, 1, :], ex, AX_X, ALU.add))
            link(dve.reciprocal(gs[:, 2, :], gs[:, 1, :]))
            link(dve.tensor_tensor(prob, ex, wide(gs[:, 2, :]), ALU.mult))
            for i in range(NT):
                this = prob[:, i, :].unsqueeze(2).broadcast_to([P, E, E])
                other = prob[:, i, :].unsqueeze(1).broadcast_to([P, E, E])
                dve.tensor_tensor(cmp_[:, 0, i, :, :], other, this, ALU.is_gt)
                last = dve.tensor_tensor(cmp_[:, 1, i, :, :], other, this, ALU.is_equal)
            link(last)
            link(dve.tensor_tensor(cmp_[:, 1, :, :, :].rearrange("p t e f -> p t (e f)"), cmp_[:, 1, :, :, :].rearrange("p t e f -> p t (e f)"),
                                   tri[:, :, :].rearrange("p e f -> p (e f)").unsqueeze(1).broadcast_to([P, NT, E * E]), ALU.mult))
            flat = [cmp_[:, i, :, :, :].rearrange("p t e f -> p (t e f)") for i in range(2)]
            link(dve.tensor_tensor(flat[0], flat[0], flat[1], ALU.add))
            link(dve.tensor_reduce(picked, cmp_[:, 0, :, :, :], AX_X, ALU.add))
            link(dve.scalar_tensor_tensor(picked, picked, 1.5, prob, ALU.is_lt, ALU.mult))
            link(dve.tensor_reduce(gs[:, 0, :], picked, AX_X, ALU.add))
            link(dve.tensor_scalar(gs[:, 1, :], gs[:, 0, :], 1e-8, None, ALU.add))
            link(dve.reciprocal(gs[:, 2, :], gs[:, 1, :]))
            link(dve.tensor_tensor(comb[:, :, :], picked, wide(gs[:, 2, :]), ALU.mult))

            def product(k):
                dve.wait_ge(sg_done, k + 1)
                if k >= 2:
                    dve.wait_ge(hl_done, k - 1)
                dve.tensor_tensor(hp[:, k % 2, :], sg[:, k % 2, :], p_sc[:, k % 2, :], ALU.mult).then_inc(hp_done, 1)

            def low(k):
                n, f = k // FF, k % FF
                dve.wait_ge(hh_done, k + 1)
                dve.tensor_tensor(hh[:, n % 2, 1, f, :], hp[:, k % 2, :], hh[:, n % 2, 0, f, :], ALU.subtract).then_inc(hl_done, 1)

            def mix(n):
                e, half = n // 2, n % 2
                dve.wait_ge(y_full, n + 1)
                if n:
                    dve.wait_ge(y_free, n)
                for i in range(4):
                    tt = half * 4 + i
                    last = dve.scalar_tensor_tensor(x_sb[:, tt, :], p_o[:, n % 2, i * P:(i + 1) * P], comb[:, tt, e:e + 1],
                                                    x_sb[:, tt, :], ALU.mult, ALU.add)
                last.then_inc(y_free, 1)

            for k in range(2 * E * FF + 1):
                if k < 2 * E * FF:
                    product(k)
                if k:
                    low(k - 1)
                if k % FF == 3 and k > FF:
                    mix(k // FF - 1)
            mix(2 * E - 1)

        @block.scalar
        def _(act):
            def copy_out(dst, key, src=lambda ps: ps):
                ps, free = misc_wait(act, key)
                act.copy(dst, src(ps)).then_inc(free, 1)

            def front0(b):
                for m in range(M0):
                    if b and m == 0:
                        act.wait_ge(k_stacked, 96 * b)
                    ps, _free = misc_wait(act, ("k0", b, m))
                    act.copy(kx[:, 0, m, :], ps).then_inc(k_hi, 1)
                for kt in range(KT):
                    copy_out(v0[:, b % 2, kt, :], ("v0", b, kt))
                copy_out(xT[:, b % 2, :], ("xT", b), lambda ps: ps[:, 0:S])
                for i in range(2):
                    if b and i == 0:
                        act.wait_ge(q_stacked, 96 * b)
                    ps, _free = misc_wait(act, ("q0", b, i))
                    act.copy(qx[:, 0, 2 * i:2 * i + 2, :].rearrange("p m n -> p (m n)"), ps).then_inc(q_hi, 1)

            def softmax(u, h, scale, before):
                for half in range(2):
                    act.wait_ge(sc_full[half], u + 1)
                    if half == 0 and before > 0:
                        act.wait_ge(av_done, before)
                    act.activation(probs[:, h % 8, half * 512:(half + 1) * 512], p_sc[:, half, :], ACT.Exp,
                                   scale=scale).then_inc(sc_free[half], 1)

            def outputs0(b, g):
                act.wait_ge(av_done, b * 2 + g + 1)
                act.copy(osb[:, 2 * g:2 * g + 2, :].rearrange("p m n -> p (m n)"), p_o[:, 0, :])
                act.copy(ssb[:, g, :], p_o[:, 1, 0:S]).then_inc(o_free, 1)

            def project0(b):
                for i in range(T):
                    copy_out(aT[:, i, :, :].rearrange("p m n -> p (m n)"), ("aT", b, i))

            for b in range(B):
                copy_out(cT[:, b * C:(b + 1) * C], ("cT", b), lambda ps: ps[0:CD, :])
            front0(0)
            for b in range(B):
                if b + 1 < B:
                    front0(b + 1)
                for h in range(H0):
                    n = b * 2 + h // 4
                    softmax(b * H0 + h, h, DH0 ** -0.5, n - 1)
                    if h == 6:
                        outputs0(b, 0)
                outputs0(b, 1)
                project0(b)

            for b in range(B):
                copy_out(xT[:, b % 2, :], ("xT", B + b), lambda ps: ps[:, 0:S])
                act.wait_ge(pwl_j, b + 1)
                act.activation(probs[:, 4, :], probs[:, 3, :], ACT.Gelu, scale=0.25).then_inc(nodes, 1)
                act.activation(probs[:, 5, :], probs[:, 3, :], ACT.Gelu, bias=quarter[:, 0:1], scale=0.25).then_inc(nodes, 1)

            act.wait_ge(ld_w2, 16 * 12)

            def front1(b):
                act.wait_ge(k_stacked, 96 * B + 48 * b)
                ps, _free = misc_wait(act, ("k1", b))
                act.activation(kx[:, 0, 0, :], ps, ACT.Identity, bias=bk1[:, 0:1]).then_inc(k_hi, 1)
                copy_out(xT[:, b % 2, :], ("xT", 2 * B + b), lambda ps: ps[:, 0:S])
                act.wait_ge(q_stacked, 96 * B + 48 * b)
                ps, _free = misc_wait(act, ("q1", b))
                act.activation(qx[:, 0, 0, :], ps[:, 0:S], ACT.Identity, bias=bq1[:, 0:1]).then_inc(q_hi, 1)

            def outputs1(b, g):
                n = 2 * B + b * 4 + g
                act.wait_ge(av_done, n + 1)
                act.copy(osb[:, g, :], p_o[:, n % 2, 0:S]).then_inc(o_free, 1)

            def project1(b):
                copy_out(aT[:, 0, 0:2, :].rearrange("p a b -> p (a b)"), ("aT1", b), lambda ps: ps[:, 0:S])
                ps, free = misc_wait(act, ("h1", b))
                act.activation(ssb[:, 0, :], ps[:, 0:S], ACT.Relu, bias=f1b1[:, 0:1])
                act.activation(ssb[:, 1, :], ps[:, S:2 * S], ACT.Relu, bias=f1b1[:, 1:2]).then_inc(free, 1)

            front1(0)
            for b in range(B):
                if b + 1 < B:
                    front1(b + 1)
                for h in range(H1):
                    n = 2 * B + b * 4 + h // 4
                    softmax(B * H0 + b * H1 + h, h, DH1 ** -0.5, n - 1)
                    if h % 4 == 2 and h > 4:
                        outputs1(b, h // 4 - 1)
                outputs1(b, 3)
                project1(b)

            for b in range(B):
                ps, _free = misc_wait(act, ("xT", 3 * B + b))
                act.copy(osb[:, b, :], ps[:, 0:S])
                act.copy(xh[:, 0, b * S:(b + 1) * S], ps[:, 0:S]).then_inc(xh_hi, 1)
            act.wait_ge(gate_d, 1)
            act.activation(lg[:, 2, :, :], lg[:, 1, :, :], ACT.Exp).then_inc(gate_e, 1)

            def high(k):
                n, f = k // FF, k % FF
                act.wait_ge(hp_done, k + 1)
                if n >= 2 and f == 0:
                    act.wait_ge(y_full, n - 1)
                act.copy(hh[:, n % 2, 0, f, :], hp[:, k % 2, :]).then_inc(hh_done, 1)

            for k in range(2 * E * FF + 1):
                if k < 2 * E * FF:
                    act.wait_ge(gu_full, k + 1)
                    act.activation(sg[:, k % 2, :], p_max[:, k % 2, :], ACT.Silu).then_inc(sg_done, 1)
                if k:
                    high(k - 1)

        @block.gpsimd
        def _(pool):
            chain = [0]

            def link(ins):
                chain[0] += 1
                ins.then_inc(pool_chain, 1)
                pool.wait_ge(pool_chain, chain[0])

            def norm(n):
                pool.wait_ge(ln_var, n + 1)
                link(pool.tensor_scalar(veps[:, n % 2, :], meanvar[:, n % 2, :, 1], EPS, None, ALU.add))
                pool.tensor_tensor(rstd[:, n % 2, :], veps[:, n % 2, :], mhalf[:, :], ALU.pow).then_inc(ln_rstd, 1)
                pool.wait_ge(ln_rstd, n + 1)

            link(pool.memset(ident[:, :], 0.0))
            link(pool.affine_select(out=ident[:, :], in_=ident[:, :], compare_op=ALU.not_equal, fill=1.0, base=0,
                                    pattern=[[-1, P]], channel_multiplier=1))
            link(pool.memset(mhalf[:, :], -0.5))
            link(pool.memset(ones[:, :], 1.0))
            pool.memset(quarter[:, :], 0.25).then_inc(consts, 1)
            pool.wait_ge(consts, 1)
            norm(0)
            for b in range(2):
                link(pool.memset(qB[SEL0:P, b, :, :], 0.0))
                link(pool.memset(kB[SEL0:P, b, :, :], 0.0))
                link(pool.affine_select(out=kB[SEL0:P, b, :, :], in_=kB[SEL0:P, b, :, :], compare_op=ALU.not_equal,
                                        fill=-1.0, base=0, pattern=[[-1, H0], [0, C]], channel_multiplier=1))
            pool.sem_inc(consts, 1)
            norm(1)
            for b in range(2):
                link(pool.memset(qS[:, b, :, :], 0.0))
                link(pool.memset(kS[:, b, :, :], 0.0))
                link(pool.affine_select(out=kS[SEL1:P, b, :, :], in_=kS[SEL1:P, b, :, :], compare_op=ALU.not_equal,
                                        fill=-1.0, base=0, pattern=[[-1, H1], [0, C]], channel_multiplier=1))
                if b == 0:
                    norm(2)
            link(pool.memset(tri[:, :, :], 1.0))
            link(pool.affine_select(out=tri[:, :, :], in_=tri[:, :, :], compare_op=ALU.is_gt, fill=0.0, base=0,
                                    pattern=[[1, E], [-1, E]], channel_multiplier=0))
            norm(3)
            pool.wait_ge(av_done, 2 * B)
            link(pool.memset(v1[:, :, :, :], 0.0))
            for b in range(2):
                link(pool.memset(v1[:, b, :, 0:VW * H1].rearrange("p k (h c) -> p k h c", c=VW)[:, :, :, DH1], 1.0))
            pool.sem_inc(consts, 1)
            for b in range(B):
                norm(B + b)
            done = 0
            for n in range(2 * B, 3 * B):
                norm(n)
                for c in range(6 * (n - 2 * B), 6 * (n - 2 * B) + 6):
                    w, e = c % 3, c // 3
                    pool.wait_ge(ld_stage[c % 2], 16 * (c // 2 + 1))
                    link(pool.tensor_copy(ew[w][:, 0, e, :], stage[:, c % 2, :]))
                    pool.tensor_tensor(ew[w][:, 1, e, :], stage[:, c % 2, :], ew[w][:, 0, e, :], ALU.subtract).then_inc(stage_free, 1)
                    pool.wait_ge(stage_free, c + 1)
            for b in range(B):
                norm(3 * B + b)

        @block.sync
        def _(sp):
            def row(v):
                return v.rearrange("(a d) -> a d", a=1).partition_broadcast(P)

            sp.dma_start(raw, t["ctx_768"].rearrange("b (k p) d -> p (b k) d", p=P)).then_inc(ld_c, 16)
            sp.dma_start(x_sb[:, :, :], t["x"].rearrange("b (i p) d -> p (b i) d", p=P)).then_inc(ld_x, 16)
            for dst, src in ((wk0, "L0_xattn_Wk"), (wv0, "L0_xattn_Wv"), (wq0, "L0_xattn_Wq")):
                sp.dma_start(dst[:, :], t[src]).then_inc(ld_w0, 16)
            sp.dma_start(wo0[:, :, :], t["L0_xattn_Wo"].rearrange("(m p) n -> p m n", p=P)).then_inc(ld_w1, 16)
            sp.dma_start(f0w1[:, :], t["L0_ffn_w1"]).then_inc(ld_w1, 16)
            sp.dma_start(f0w2[:, :, :], t["L0_ffn_w2"].rearrange("(m p) n -> p m n", p=P)).then_inc(ld_w1, 16)
            sp.dma_start(f0b1[:, :], t["L0_ffn_b1"]).then_inc(ld_w1, 16)
            sp.dma_start(bo0[:, :], row(t["L0_xattn_bo"])).then_inc(ld_w1, 16)
            sp.dma_start(f0b2[:, :], row(t["L0_ffn_b2"])).then_inc(ld_w1, 16)

            def stack0(b):
                for src, what, lo_sem, a, bb in ((kx, "k0", k_stacked, kA, kB), (qx, "q0", q_stacked, qA, qB)):
                    for i in range(M0 if what == "k0" else 2):
                        misc_done(sp, (what, b, i))
                    if b < 2 and what == "k0":
                        sp.wait_ge(consts, 2)
                    for i in range(2):
                        rows = slice(64 * i, 64 * i + 64)
                        low = 0 if what == "k0" else 1
                        sp.dma_start(a[0:64, b % 2, i::2, :], src[rows, 0, :, :]).then_inc(lo_sem, 16)
                        sp.dma_start(a[64:128, b % 2, i::2, :], src[rows, low, :, :]).then_inc(lo_sem, 16)
                        sp.dma_start(bb[0:64, b % 2, i::2, :], src[rows, 1 - low, :, :]).then_inc(lo_sem, 16)

            stack0(0)
            for dst, src in ((wq1, "L1_xattn_Wq"), (wk1, "L1_xattn_Wk"), (wv1, "L1_xattn_Wv"), (f1w1, "L1_xattn_W1"),
                             (wg, "L1_ffn_Wg")):
                sp.dma_start(dst[:, :], t[src]).then_inc(ld_w2, 16)
            sp.dma_start(f1w2[:, :, :], t["L1_xattn_W2"].rearrange("(m p) n -> p m n", p=P)).then_inc(ld_w2, 16)
            sp.dma_start(f1b1[:, :], t["L1_xattn_b1"]).then_inc(ld_w2, 16)
            sp.dma_start(bq1[:, :], t["L1_xattn_bq"]).then_inc(ld_w2, 16)
            sp.dma_start(bk1[:, :], t["L1_xattn_bk"]).then_inc(ld_w2, 16)
            sp.dma_start(bv1[:, :], row(t["L1_xattn_bv"])).then_inc(ld_w2, 16)
            sp.dma_start(f1b2[:, :], row(t["L1_xattn_b2"])).then_inc(ld_w2, 16)
            sp.sem_inc(ld_w2, 16)
            for b in range(1, B):
                stack0(b)

            experts = [t["L1_ffn_W1"], t["L1_ffn_W3"], t["L1_ffn_W2"].rearrange("e (f p) d -> e p f d", p=P)]

            def stage_in(c):
                w, e = c % 3, c // 3
                if c >= 2:
                    sp.wait_ge(stage_free, c - 1)
                dst = stage[:, c % 2, :]
                if w == 2:
                    dst = dst.rearrange("p (f d) -> p f d", f=FF)
                sp.dma_start(dst, experts[w][e]).then_inc(ld_stage[c % 2], 16)

            def stack1(b):
                for src, key, bounced, scr, dst, sm, parts in (
                        (kx, "k1", k_bounced, dk, kS, k_stacked, (0, 1, 0)), (qx, "q1", q_bounced, dq, qS, q_stacked, (0, 0, 1))):
                    n = C if key == "k1" else S
                    misc_done(sp, (key, b))
                    sp.dma_start(scr[b], src[:, :, 0, :]).then_inc(bounced, 16)
                    sp.wait_ge(bounced, 16 * (b + 1))
                    view = scr[b].rearrange("(h d) s n -> s d h n", d=DH1)
                    for i, part in enumerate(parts):
                        sp.dma_start(dst[DH1 * i:DH1 * (i + 1), b % 2, :, :], view[part]).then_inc(sm, 16)

            sp.wait_ge(consts, 3)
            stage_in(0)
            stage_in(1)
            stack1(0)
            done = 2
            for b in range(1, B):
                while done < 6 * b:
                    stage_in(done)
                    done += 1
                stack1(b)
            while done < 24:
                stage_in(done)
                done += 1
            for half in range(2):
                sp.wait_ge(y_free, 2 * E - 1 + half)
                sp.dma_start(out.rearrange("b (i p) d -> p (b i) d", p=P)[:, half * 4:half * 4 + 4, :],
                             x_sb[:, half * 4:half * 4 + 4, :]).then_inc(stored, 16)
            sp.wait_ge(stored, 32)


_INS = ['x', 'ctx_768', 'L0_xattn_Wq', 'L0_xattn_Wk', 'L0_xattn_Wv', 'L0_xattn_Wo', 'L0_xattn_bo', 'L0_ffn_w1', 'L0_ffn_b1',
        'L0_ffn_w2', 'L0_ffn_b2', 'L1_xattn_Wq', 'L1_xattn_bq', 'L1_xattn_Wk', 'L1_xattn_bk', 'L1_xattn_Wv', 'L1_xattn_bv',
        'L1_xattn_W1', 'L1_xattn_b1', 'L1_xattn_W2', 'L1_xattn_b2', 'L1_ffn_Wg', 'L1_ffn_W1', 'L1_ffn_W2', 'L1_ffn_W3']


def kernel(**inputs):
    import numpy as _np
    import concourse.bacc as _bacc
    from concourse import mybir as _mybir
    from concourse.bass_utils import run_bass_kernel_spmd as _run

    nc = _bacc.Bacc("TRN2", target_bir_lowering=False, num_devices=1)
    arrays, aps = {}, {}
    for name in _INS:
        a = _np.asarray(inputs[name])
        if name in ("L0_ffn_b1", "L1_xattn_b1", "L1_xattn_bq", "L1_xattn_bk"):
            a = a.reshape(-1, P).T
        a = _np.ascontiguousarray(a)
        arrays[f"in_{name}_dram"] = a
        aps[name] = nc.dram_tensor(f"in_{name}_dram", a.shape, _mybir.dt.from_np(a.dtype), kind="ExternalInput").ap()
    out = nc.dram_tensor("out_dram", (B, S, P), _mybir.dt.float32, kind="ExternalOutput").ap()
    build(nc, aps, out)
    r = _run(nc, [arrays], core_ids=[0])
    return r.results[0]["out_dram"]
```

```python
from contextlib import ExitStack

import concourse.bass as bass
from concourse import mybir

ALU = mybir.AluOpType
ACT = mybir.ActivationFunctionType
F32 = mybir.dt.float32
F16 = mybir.dt.float16
AX_X = mybir.AxisListType.X

P = 128
B = 4
S = 256
T = 2
C = 512
CD = 96
KT = C // P
H0, DH0 = 8, 64
H1, DH1 = 16, 8
M0 = H0 * DH0 // P
FF = 4
E = 8
MAGIC = 12582912.0
FIX = 256.0
EPS = 1e-5
SEL0 = 64
SEL1 = 96
VW = DH1 + 1


NODE = 2 * S


def schedule():
    order = []

    def queries(kind, ln, b):
        return [("ln", ln), ("xT", ln), ("q" + kind, b)] if kind == "1" else [("ln", ln), ("xT", ln), ("q0", b, 0), ("q0", b, 1)]

    def keys0(b):
        return [("k0", b, m) for m in range(M0)]

    def values0(b):
        return [("v0", b, kt) for kt in range(KT)]

    def project0(b):
        return [(kind, b, i) for i in range(T) for kind in ("sT", "oT", "aT", "y0")]

    def feed0(b):
        steps = [("ln", ln_ffn(b)), ("xT", ln_ffn(b))]
        for i in range(2):
            steps += [("up0", b, i), ("floor", b, i), ("nodes", b, i), ("frac", b, i), ("slope", b, i), ("interp", b, i)]
        return steps + [("down0", b)]

    def project1(b):
        return [("oT1", b, 0), ("oT1", b, 1), ("aT1", b), ("h1", b), ("y1", b)]

    def tokens(b):
        return [("ln", ln_exp(b)), ("xT", ln_exp(b)), ("logits", b)]

    def maxima(layer, b):
        return [("max", layer, b, h) for h in range(H0 if layer == 0 else H1)]

    def sums(ahead):
        return [("sum", b, 4 * g + j) for _, layer, b, g, c in ahead if layer == 0 for j in ((0, 1), (2,), (3,), ())[c]]

    chunks = []

    def iteration(layer, b, nxt, fill, proj, late, last):
        heads = H0 if layer == 0 else H1
        first_late = 4
        for h in range(heads):
            order.append(("sc", layer, b, h))
            if chunks:
                order.append(chunks.pop(0))
                order.extend(sums(chunks[:1]))
            if h >= 2:
                n = -(-len(nxt) // (heads - h))
                order.extend(nxt[:n])
                del nxt[:n]
            n = -(-len(fill) // max(1, heads - 2 - h))
            order.extend(fill[:n])
            del fill[:n]
            if first_late <= h < 7:
                n = -(-len(proj) // (7 - h))
                order.extend(proj[:n])
                del proj[:n]
            if h >= first_late:
                n = -(-len(late) // (heads - h))
                order.extend(late[:n])
                del late[:n]
            if h >= heads - 2:
                n = -(-len(last) // (heads - h))
                order.extend(last[:n])
                del last[:n]
            if h % 4 == 3:
                chunks.extend(("av", layer, b, h // 4, c) for c in range(4))
                order.extend(sums(chunks[:1]))
        order.extend(nxt + fill + late)

    for b in range(B):
        order.append(("cT", b))
    order.extend([("ln", 0)] + keys0(0) + queries("0", 0, 0)[1:] + [("init", 0), ("stack0", 0)] + values0(0) + keys0(1) + queries("0", 1, 1))
    order.extend(maxima(0, 0) + [("rows", 0, 0), ("init", 1)])
    for b in range(B):
        order.append(("stack0", b + 1) if b + 1 < B else ("stack1", 0))
        fill = feed0(b - 2) if b >= 2 else []
        proj = project0(b - 1) if b else []
        late, last = [], []
        if b + 1 < B:
            late += values0(b + 1)
        else:
            late += [("init", 2), ("v1", 0)]
        if b + 2 < B:
            late += keys0(b + 2) + queries("0", b + 2, b + 2)
        else:
            late += [("k1", b - 2)]
            last += queries("1", ln_att1(b - 2), b - 2)
        if b + 1 == B:
            last.append(("init", 3))
        iteration(0, b, maxima(0, b + 1) if b + 1 < B else maxima(1, 0), fill, proj, late, last)
        order.append(("rows", 0, b + 1) if b + 1 < B else ("rows", 1, 0))
    for b in range(B):
        if b + 1 < B:
            order.append(("stack1", b + 1))
        fill = feed0(b + 2) if b + 2 < B else []
        proj = project0(B - 1) if b == 0 else project1(b - 1)[:2]
        late, last = project1(b - 1)[2:] if b else [], []
        if b + 1 < B:
            late.append(("v1", b + 1))
        if b + 2 < B:
            late += [("k1", b + 2)]
            last += queries("1", ln_att1(b + 2), b + 2)
        if b + 1 == B:
            late += tokens(0) + tokens(1) + [("route", 0)]
        else:
            for i in range(8):
                c = 8 * b + i
                late.insert(2 * i, ("stage", c))
                if c:
                    late.insert(2 * i + 1, ("split", c - 1))
        if b + 1 == B:
            late.insert(0, ("split", 3 * E - 1))
        iteration(1, b, maxima(1, b + 1) if b + 1 < B else [], fill, proj, late, last)
        if b + 1 < B:
            order.append(("rows", 1, b + 1))
    order.extend(chunks)

    rest = project1(B - 1) + tokens(2) + tokens(3) + [("route", 1)]
    for n in range(2 * E + 1):
        for f in range(FF):
            if n < 2 * E:
                order.append(("gu", n, f))
            if n and f >= 2:
                order.extend([("dn", n - 1, 2 * (f - 2)), ("dn", n - 1, 2 * (f - 2) + 1)])
            if n < 2 * E or f == 0:
                order.append(("act", n, f))
            if rest:
                order.extend(rest[:1])
                del rest[:1]
    order.append(("mix", 2 * E - 1))
    return order


def ln_ffn(b):
    return B + 2 * b


def ln_att1(b):
    return B + 2 * b + 1


def ln_exp(b):
    return 3 * B + b


def build(nc, t, out):
    ctx = ExitStack()
    with ctx:
        def sb(name, shape, dt=F32):
            return ctx.enter_context(nc.sbuf_tensor(name, shape, dt))

        def sem(name):
            return ctx.enter_context(nc.semaphore(name))

        def sems(name, n):
            return [sem(f"{name}{i}") for i in range(n)]

        ident = sb("ident", [P, P])
        x_sb = sb("x_sb", [P, B * T, P])
        cT = sb("cT", [CD, B * C])
        wq0 = sb("wq0", [P, H0 * DH0])
        wk0 = sb("wk0", [CD, H0 * DH0])
        wv0 = sb("wv0", [CD, H0 * DH0])
        wo0 = sb("wo0", [P, M0, P])
        f0w1 = sb("f0w1", [P, FF * P])
        f0w2 = sb("f0w2", [P, FF, P])
        f0b1 = sb("f0b1", [P, FF])
        wq1 = sb("wq1", [P, P])
        wk1 = sb("wk1", [CD, P])
        wv1 = sb("wv1", [CD, P])
        bq1 = sb("bq1", [P, 1])
        bk1 = sb("bk1", [P, 1])
        f1w1 = sb("f1w1", [P, 2 * P])
        f1w2 = sb("f1w2", [P, 2, P])
        f1b1 = sb("f1b1", [P, 2])
        wg = sb("wg", [P, E])
        bo0 = sb("bo0", [P, P])
        f0b2 = sb("f0b2", [P, P])
        bv1 = sb("bv1", [P, P])
        f1b2 = sb("f1b2", [P, P])
        region = sb("region", [P, 24576], F16)
        kA = region[:, 0:8192].rearrange("p (b h k) -> p b h k", b=2, h=H0)
        kB = region[:, 8192:16384].rearrange("p (b h k) -> p b h k", b=2, h=H0)
        qA = region[:, 16384:20480].rearrange("p (b h k) -> p b h k", b=2, h=H0)
        qB = region[:, 20480:24576].rearrange("p (b h k) -> p b h k", b=2, h=H0)
        ew = [region[:, 8192 * i:8192 * (i + 1)].rearrange("p (s e n) -> p s e n", s=2, e=E) for i in range(3)]
        kS = sb("kS", [P, 2, H1, C], F16)
        qS = sb("qS", [P, 2, H1, S], F16)
        kx = sb("kx", [P, 2, M0, C], F16)
        qx = sb("qx", [P, 2, M0, S], F16)
        v0 = sb("v0", [P, 2, KT, H0 * DH0])
        VR = VW * H1 + 32 - VW
        v1 = v0[:, 0, :, :].rearrange("p k n -> p (k n)")[:, 0:2 * KT * VR].rearrange("p (b k n) -> p b k n", b=2, k=KT)
        stage = v0[:, 1, 0:2, :]
        probs = sb("probs", [P, 8, KT * S])
        raw = probs[:, 0:2, :].rearrange("p a b -> p (a b)")[:, 0:B * KT * CD].rearrange("p (c d) -> p c d", d=CD)
        xn = sb("xn", [P, 2, T, P])
        xT = sb("xT", [P, 2, S])
        xh = qS[:, 0, 0:8, :].rearrange("p h n -> p (h n)").rearrange("p (s n) -> p s n", s=2)
        cmp_ = kS[:, 0, 0:4, :].rearrange("p h n -> p (h n)").bitcast(F32).rearrange("p (s t e f) -> p s t e f", s=2, t=B * T, e=E)
        mx = sb("mx", [P, 2, T, H1])
        stats = sb("stats", [P, T, 6])
        meanvar = sb("meanvar", [P, 2, T, 2])
        veps = sb("veps", [P, 2, T])
        rstd = sb("rstd", [P, 2, T])
        mhalf = sb("mhalf", [P, T])
        ones = sb("ones", [P, 32])
        quarter = sb("quarter", [P, 1])
        osb = sb("osb", [P, 4, S])
        ssb = sb("ssb", [P, 2, S])
        rden = sb("rden", [P, T, H1])
        a0 = sb("a0", [P, M0 * P])
        aT = sb("aT", [P, M0 * P])
        ytmp = sb("ytmp", [P, T, P])
        lg = kS[:, 0, 4:6, :].rearrange("p h n -> p (h n)").bitcast(F32).rearrange("p (i t e) -> p i t e", i=8, t=B * T)
        gs = sb("gs", [P, 4, B * T])
        tri = sb("tri", [P, E, E])
        comb = sb("comb", [P, B * T, E])
        fixed = [v.rearrange("p (i n) -> p i n", n=NODE) for v in (
            kS[:, 1, :, :].rearrange("p h n -> p (h n)").bitcast(F32), region[:, 16384:24576].bitcast(F32))]
        psums = sb("psums", [P, 4, S])
        mrow = sb("mrow", [H1, S], F16)
        sg = probs[:, 0, :].rearrange("p (a b) -> p a b", a=2)
        hp = probs[:, 1, :].rearrange("p (a b) -> p a b", a=2)
        hh = probs[:, 2:6, :].bitcast(F16).rearrange("p (b s) (f n) -> p b s f n", b=2, f=FF)

        p_max = ctx.enter_context(nc.psum_tensor("p_max", [P, 2, 512], F32))
        p_sc = ctx.enter_context(nc.psum_tensor("p_sc", [P, 2, 512], F32))
        p_o = ctx.enter_context(nc.psum_tensor("p_o", [P, 2, 512], F32))
        p_misc = ctx.enter_context(nc.psum_tensor("p_misc", [P, 2, 512], F32))

        dk = nc.dram_tensor("k_scratch", (B, P, 2, C), F16).ap()
        dq = nc.dram_tensor("q_scratch", (B, P, 2, S), F16).ap()

        ld_x, ld_c, ld_w0, ld_w1, ld_w2 = (sem(f"ld_{n}") for n in ("x", "c", "w0", "w1", "w2"))
        ld_stage = sems("ld_stage", 2)
        stage_free = sem("stage_free")
        const_pe, zero_kb, stack_init = sem("const_pe"), sem("zero_kb"), sem("stack_init")
        misc_full = sems("misc_full", 2)
        misc_free = sems("misc_free", 2)
        ln_var, ln_rstd, ln_xn = sem("ln_var"), sem("ln_rstd"), sem("ln_xn")
        k_hi, q_hi = sem("k_hi"), sem("q_hi")
        k_stacked, q_stacked = sem("k_stacked"), sem("q_stacked")
        k_bounced, q_bounced = sem("k_bounced"), sem("q_bounced")
        max_full, max_free = sems("max_full", 2), sems("max_free", 2)
        rows_set = sem("rows_set")
        sc_full, sc_free = sems("sc_full", 2), sems("sc_free", 2)
        sums_set = sem("sums_set")
        av_done, o_free = sem("av_done"), sem("o_free")
        breaks, nodes, slopes, hidden = sem("breaks"), sem("nodes"), sem("slopes"), sem("hidden")
        logits_set, gate_dif, gate_exp, xh_hi = sem("logits_set"), sem("gate_dif"), sem("gate_exp"), sem("xh_hi")
        gu_full, sg_done, hp_done, hh_done, hl_done = (sem(n) for n in ("gu_full", "sg_done", "hp_done", "hh_done", "hl_done"))
        y_full, y_free = sem("y_full"), sem("y_free")
        dve_chain, pool_chain = sem("dve_chain"), sem("pool_chain")
        stored = sem("stored")
        order = schedule()
        ln_batch = {b: b for b in range(B)}
        for b in range(B):
            ln_batch.update({ln_ffn(b): b, ln_att1(b): b, ln_exp(b): b})

        misc = {}

        def misc_take(pe, key):
            n = len(misc)
            bank, use = n % 2, n // 2 + 1
            if use > 1:
                pe.wait_ge(misc_free[bank], use - 1)
            misc[key] = (bank, use)
            return p_misc[:, bank, :], misc_full[bank]

        def misc_wait(eng, key):
            bank, use = misc[key]
            eng.wait_ge(misc_full[bank], use)
            return p_misc[:, bank, :], misc_free[bank]

        def misc_done(eng, key):
            bank, use = misc[key]
            eng.wait_ge(misc_free[bank], use)

        block = ctx.enter_context(nc.Block())

        def head_number(layer, b, h):
            return b * H0 + h if layer == 0 else B * H0 + b * H1 + h

        def group_number(layer, b, g):
            return b * 2 + g if layer == 0 else B * 2 + b * 4 + g

        @block.tensor
        def _(pe):
            def transposes(key, parts):
                ps, full = misc_take(pe, key)
                at = 0
                for src in parts:
                    k, m = src.shape
                    last = pe.transpose(ps[0:m, at:at + k], src, ident[0:k, 0:k])
                    at += k
                last.then_inc(full, 1)

            def context(b):
                if b == 0:
                    pe.wait_ge(ld_c, 16)
                    pe.wait_ge(const_pe, 1)
                transposes(("cT", b), [raw[:, b * KT + i, :] for i in range(KT)])

            def keys0(b, m):
                if b == 0 and m == 0:
                    pe.wait_ge(ld_w0, 48)
                if m == 0:
                    misc_done(pe, ("cT", b))
                ps, full = misc_take(pe, ("k0", b, m))
                pe.matmul(ps, wk0[:, m * P:(m + 1) * P], cT[:, b * C:(b + 1) * C], start=True, stop=True).then_inc(full, 1)

            def values0(b, kt):
                ps, full = misc_take(pe, ("v0", b, kt))
                pe.matmul(ps, cT[:, b * C + kt * P:b * C + (kt + 1) * P], wv0[:, :], start=True, stop=True).then_inc(full, 1)

            def xt(n):
                pe.wait_ge(ln_xn, n + 1)
                transposes(("xT", n), [xn[:, n % 2, i, :] for i in range(T)])

            def queries0(b, i):
                misc_done(pe, ("xT", b))
                ps, full = misc_take(pe, ("q0", b, i))
                for m in (2 * i, 2 * i + 1):
                    last = pe.matmul(ps[:, (m % 2) * S:(m % 2 + 1) * S], wq0[:, m * P:(m + 1) * P], xT[:, b % 2, :],
                                     start=True, stop=True)
                last.then_inc(full, 1)

            def maxima(layer, b, h):
                u = head_number(layer, b, h)
                if h == 0:
                    stacked = 96 * (b + 1) if layer == 0 else 96 * B + 48 * (b + 1)
                    pe.wait_ge(k_stacked, stacked)
                    pe.wait_ge(q_stacked, stacked)
                q, k = (qA[:, b % 2, h, :], kA[:, b % 2, h, :]) if layer == 0 else (
                    qS[0:SEL1, b % 2, h, :], kS[0:SEL1, b % 2, h, :])
                for i in range(T):
                    if u:
                        pe.wait_ge(max_free[i], u)
                    pe.matmul(p_max[:, i, :], q[:, i * P:(i + 1) * P], k, start=True, stop=True).then_inc(max_full[i], 1)

            def rows(layer, b):
                h = H0 if layer == 0 else H1
                u = head_number(layer, b, h)
                pe.wait_ge(max_free[0], u)
                pe.wait_ge(max_free[1], u)
                transposes(("rows", layer, b), [mx[:, b % 2, i, 0:h] for i in range(T)])

            def scores(layer, b, h):
                u = head_number(layer, b, h)
                if h == 0 or h == 4:
                    pe.wait_ge(rows_set, 2 * (b + B * layer) + h // 4 + 1)
                if layer == 0:
                    if b == 0 and h == 0:
                        pe.wait_ge(stack_init, 1)
                    pairs = [(kA[:, b % 2, h, :], qA[:, b % 2, h, :]), (kB[:, b % 2, h, :], qB[:, b % 2, h, :])]
                else:
                    pairs = [(kS[:, b % 2, h, :], qS[:, b % 2, h, :])]
                for half in range(2):
                    if u:
                        pe.wait_ge(sc_free[half], u)
                    for j in range(2):
                        kt = 2 * half + j
                        for i, (k, q) in enumerate(pairs):
                            last = pe.matmul(p_sc[:, half, j * S:(j + 1) * S], k[:, kt * P:(kt + 1) * P], q,
                                             start=(i == 0), stop=(i == len(pairs) - 1))
                    last.then_inc(sc_full[half], 1)

            def attend(layer, b, g, c):
                n = group_number(layer, b, g)
                u = head_number(layer, b, 4 * (g + 1))
                if c == 0:
                    pe.wait_ge(sc_free[0], u)
                    pe.wait_ge(sc_free[1], u)
                    if n:
                        pe.wait_ge(o_free, n if layer == 0 or n == 2 * B else n - 1)
                if layer == 0:
                    m = c // 2
                    for kt in (2 * (c % 2), 2 * (c % 2) + 1):
                        for i in range(2):
                            h = 4 * g + 2 * m + i
                            pe.matmul(p_o[64 * i:64 * i + 64, 0, m * S:(m + 1) * S], v0[:, b % 2, kt, h * DH0:(h + 1) * DH0],
                                      probs[:, h % 8, kt * S:(kt + 1) * S], start=(kt == 0), stop=(kt == KT - 1))
                    if c == 3:
                        pe.wait_ge(sums_set, u)
                        if n == 0:
                            pe.wait_ge(const_pe, 2)
                        for j in range(4):
                            last = pe.matmul(p_o[32 * j:32 * j + 32, 1, 0:S], ones[:, :], psums[:, j, :], start=True, stop=True,
                                             tile_position=(0, 32 * j))
                        last.then_inc(av_done, 1)
                else:
                    for j in range(4):
                        h = 4 * g + j
                        last = pe.matmul(p_o[32 * j:32 * j + 32, n % 2, 0:S], v1[:, b % 2, c, h * VW:h * VW + 32],
                                         probs[:, h % 8, c * S:(c + 1) * S], start=(c == 0), stop=(c == KT - 1),
                                         tile_position=(0, 32 * j))
                    if c == 3:
                        last.then_inc(av_done, 1)

            def sums_t(b, i):
                if i == 0:
                    pe.wait_ge(o_free, 2 * (b + 1))
                transposes(("sT", b, i), [ssb[:, g, i * P:(i + 1) * P] for g in range(2)])

            def heads_t(b, i):
                transposes(("oT", b, i), [osb[:, m, i * P:(i + 1) * P] for m in range(M0)])

            def heads_back(b, i):
                misc_done(pe, ("oT", b, i))
                transposes(("aT", b, i), [a0[:, m * P:(m + 1) * P] for m in range(M0)])

            def project0(b, i):
                if b == 0 and i == 0:
                    pe.wait_ge(ld_w1, 16 * 6)
                misc_done(pe, ("aT", b, i))
                ps, full = misc_take(pe, ("y0", b, i))
                for m in range(M0):
                    last = pe.matmul(ps[:, 0:P], aT[:, m * P:(m + 1) * P], wo0[:, m, :], start=(m == 0), stop=(m == M0 - 1))
                last.then_inc(full, 1)

            def up0(b, i):
                n = ln_ffn(b)
                misc_done(pe, ("xT", n))
                ps, full = misc_take(pe, ("h0", b, i))
                for f in (2 * i, 2 * i + 1):
                    last = pe.matmul(ps[:, (f % 2) * S:(f % 2 + 1) * S], f0w1[:, f * P:(f + 1) * P], xT[:, n % 2, :],
                                     start=True, stop=True)
                last.then_inc(full, 1)

            def down0(b):
                pe.wait_ge(hidden, 2 * (b + 1))
                ps, full = misc_take(pe, ("z0", b))
                hid = fixed[b // 2][:, 6:8, :].rearrange("p i n -> p (i n)")
                for i in range(T):
                    for f in range(FF):
                        last = pe.matmul(ps[:, i * P:(i + 1) * P], hid[:, f * S + i * P:f * S + (i + 1) * P], f0w2[:, f, :],
                                         start=(f == 0), stop=(f == FF - 1))
                last.then_inc(full, 1)

            def keys1(b):
                if b == 0:
                    pe.wait_ge(ld_w2, 16 * 11)
                ps, full = misc_take(pe, ("k1", b))
                pe.matmul(ps, wk1[:, :], cT[:, b * C:(b + 1) * C], start=True, stop=True).then_inc(full, 1)

            def values1(b):
                ps, full = misc_take(pe, ("v1", b))
                for kt in range(KT):
                    last = pe.matmul(ps[:, kt * P:(kt + 1) * P], cT[:, b * C + kt * P:b * C + (kt + 1) * P], wv1[:, :],
                                     start=True, stop=True)
                last.then_inc(full, 1)

            def queries1(b):
                n = ln_att1(b)
                misc_done(pe, ("xT", n))
                ps, full = misc_take(pe, ("q1", b))
                pe.matmul(ps[:, 0:S], wq1[:, :], xT[:, n % 2, :], start=True, stop=True).then_inc(full, 1)

            def heads_t1(b, i):
                if i == 0:
                    pe.wait_ge(o_free, 2 * B + 4 * (b + 1))
                transposes(("oT1", b, i), [osb[:, g, i * P:(i + 1) * P] for g in range(4)])

            def heads_back1(b):
                misc_done(pe, ("oT1", b, 0))
                misc_done(pe, ("oT1", b, 1))
                transposes(("aT1", b), [a0[:, i * P:(i + 1) * P] for i in range(T)])

            def up1(b):
                misc_done(pe, ("aT1", b))
                ps, full = misc_take(pe, ("h1", b))
                for f in range(2):
                    last = pe.matmul(ps[:, f * S:(f + 1) * S], f1w1[:, f * P:(f + 1) * P], aT[:, 0:S], start=True, stop=True)
                last.then_inc(full, 1)

            def down1(b):
                misc_done(pe, ("h1", b))
                ps, full = misc_take(pe, ("y1", b))
                for i in range(T):
                    for f in range(2):
                        last = pe.matmul(ps[:, i * P:(i + 1) * P], ssb[:, f, i * P:(i + 1) * P], f1w2[:, f, :],
                                         start=(f == 0), stop=(f == 1))
                last.then_inc(full, 1)

            def logits(b):
                n = ln_exp(b)
                misc_done(pe, ("xT", n))
                ps, full = misc_take(pe, ("logits", b))
                for i in range(T):
                    last = pe.matmul(ps[:, i * E:(i + 1) * E], xT[:, n % 2, i * P:(i + 1) * P], wg[:, :], start=True, stop=True)
                last.then_inc(full, 1)

            def gate_up(n, f):
                half, e = n // E, n % E
                k = n * FF + f
                if f == 0 and e == 0:
                    misc_done(pe, ("xT", ln_exp(2 * half)))
                    misc_done(pe, ("xT", ln_exp(2 * half + 1)))
                if f == 0 and half == 0:
                    pe.wait_ge(stage_free, 2 * (e + 1))
                if k == 0:
                    for i in range(2):
                        pe.wait_ge(max_free[i], B * (H0 + H1))
                        pe.wait_ge(sc_free[i], B * (H0 + H1))
                if k >= 2:
                    pe.wait_ge(hp_done, k - 1)
                for ps, w in ((p_max, ew[0]), (p_sc, ew[1])):
                    for i, (ws, xs) in enumerate(((0, 0), (0, 1), (1, 0))):
                        last = pe.matmul(ps[:, f % 2, :], w[:, ws, e, f * P:(f + 1) * P], xh[:, xs, half * C:(half + 1) * C],
                                         start=(i == 0), stop=(i == 2))
                last.then_inc(gu_full, 1)

            def down(n, i):
                half, e = n // E, n % E
                if i == 0:
                    if half == 0:
                        pe.wait_ge(stage_free, 2 * E + e + 1)
                    pe.wait_ge(hl_done, FF * (n + 1))
                    if n == 0:
                        pe.wait_ge(o_free, 6 * B)
                    if n >= 2:
                        pe.wait_ge(y_free, n - 1)
                at = 0
                for f in range(FF):
                    for hs, ws in ((0, 0), (0, 1), (1, 0)):
                        last = pe.matmul(p_o[:, n % 2, i * P:(i + 1) * P], hh[:, n % 2, hs, f, i * P:(i + 1) * P],
                                         ew[2][:, ws, e, f * P:(f + 1) * P], start=(at == 0), stop=(at == 3 * FF - 1))
                        at += 1
                if i == 3:
                    last.then_inc(y_full, 1)

            steps = {"cT": context, "k0": keys0, "v0": values0, "xT": xt, "q0": queries0, "max": maxima, "rows": rows, "sc": scores,
                     "av": attend, "sT": sums_t, "oT": heads_t, "aT": heads_back, "y0": project0, "up0": up0, "down0": down0,
                     "k1": keys1, "v1": values1, "q1": queries1, "oT1": heads_t1, "aT1": heads_back1, "h1": up1, "y1": down1,
                     "logits": logits, "gu": gate_up, "dn": down}
            for kind, *at in order:
                if kind in steps:
                    steps[kind](*at)

        @block.vector
        def _(dve):
            chain = [0]

            def link(ins):
                chain[0] += 1
                ins.then_inc(dve_chain, 1)
                dve.wait_ge(dve_chain, chain[0])

            def norm(n):
                b = ln_batch[n]
                if n == 0:
                    dve.wait_ge(ld_x, 16)
                for i in range(T):
                    last = dve.bn_stats(stats[:, i, :], x_sb[:, b * T + i, :])
                link(last)
                for i in range(T):
                    last = dve.bn_aggr(meanvar[:, n % 2, i, :], stats[:, i, :])
                last.then_inc(ln_var, 1)
                dve.wait_ge(ln_var, n + 1)

            def normed(n):
                b = ln_batch[n]
                dve.wait_ge(ln_rstd, n + 1)
                for i in range(T):
                    last = dve.tensor_scalar(xn[:, n % 2, i, :], x_sb[:, b * T + i, :], meanvar[:, n % 2, i, 0:1],
                                             rstd[:, n % 2, i:i + 1], ALU.subtract, ALU.mult)
                last.then_inc(ln_xn, 1)

            def xt(n):
                normed(n)
                if n >= ln_exp(0):
                    b = n - ln_exp(0)
                    dve.wait_ge(xh_hi, b + 1)
                    ps, free = misc_wait(dve, ("xT", n))
                    dve.tensor_tensor(xh[:, 1, b * S:(b + 1) * S], ps[:, 0:S], xh[:, 0, b * S:(b + 1) * S], ALU.subtract).then_inc(free, 1)

            def keys0(b, m):
                dve.wait_ge(k_hi, b * M0 + m + 1)
                ps, free = misc_wait(dve, ("k0", b, m))
                dve.tensor_tensor(kx[:, 1, m, :], ps, kx[:, 0, m, :], ALU.subtract).then_inc(free, 1)

            def queries0(b, i):
                dve.wait_ge(q_hi, b * 2 + i + 1)
                ps, free = misc_wait(dve, ("q0", b, i))
                dve.tensor_tensor(qx[:, 1, 2 * i:2 * i + 2, :].rearrange("p m n -> p (m n)"), ps,
                                  qx[:, 0, 2 * i:2 * i + 2, :].rearrange("p m n -> p (m n)"), ALU.subtract).then_inc(free, 1)

            def maxima(layer, b, h):
                u = head_number(layer, b, h)
                for i in range(T):
                    dve.wait_ge(max_full[i], u + 1)
                    dve.tensor_reduce(mx[:, b % 2, i, h:h + 1], p_max[:, i, :], AX_X, ALU.max).then_inc(max_free[i], 1)

            def rows(layer, b):
                heads, dst = (H0, qB[SEL0:SEL0 + H0, b % 2, :, :]) if layer == 0 else (H1, qS[SEL1:SEL1 + H1, b % 2, :, :])
                ps, free = misc_wait(dve, ("rows", layer, b))
                dve.tensor_copy(mrow[0:heads, :], ps[0:heads, 0:S]).then_inc(free, 1)
                misc_done(dve, ("rows", layer, b))
                for lo, hi in ((0, 4), (4, heads)):
                    src = mrow[0:heads, :].unsqueeze(1).broadcast_to([heads, hi - lo, S])
                    dve.tensor_copy(dst[:, lo:hi, :], src).then_inc(rows_set, 1)
                dve.wait_ge(rows_set, 2 * (b + B * layer) + 2)

            def sums_t(b, i):
                ps, free = misc_wait(dve, ("sT", b, i))
                dve.reciprocal(rden[:, i, 0:H0], ps[:, 0:2 * P].rearrange("p (h r) -> p h r", r=32)[:, :, 0]).then_inc(free, 1)
                misc_done(dve, ("sT", b, i))

            def heads_t(b, i):
                ps, free = misc_wait(dve, ("oT", b, i))
                dve.tensor_tensor(a0[:, :].rearrange("p (h d) -> p h d", h=H0), ps.rearrange("p (h d) -> p h d", h=H0),
                                  rden[:, i, 0:H0].unsqueeze(2).broadcast_to([P, H0, DH0]), ALU.mult).then_inc(free, 1)

            def add_to_x(b, i, key, bias, at, last_of):
                ps, free = misc_wait(dve, key)
                ins = dve.tensor_tensor(ytmp[:, i, :], ps[:, at:at + P], bias, ALU.add)
                if last_of:
                    ins.then_inc(free, 1)
                    misc_done(dve, key)
                else:
                    link(ins)
                link(dve.tensor_tensor(x_sb[:, b * T + i, :], x_sb[:, b * T + i, :], ytmp[:, i, :], ALU.add))

            def project0(b, i):
                if b == 0 and i == 0:
                    dve.wait_ge(ld_w1, 16 * 6)
                add_to_x(b, i, ("y0", b, i), bo0[:, :], 0, True)

            def temps(b):
                return [fixed[b // 2][:, i, :] for i in range(6)]

            def fix(b, i):
                A, N = temps(b)[0:2]
                ps, free = misc_wait(dve, ("h0", b, i))
                for j in range(2):
                    f = 2 * i + j
                    last = dve.tensor_scalar(A[:, j * S:(j + 1) * S], ps[:, j * S:(j + 1) * S], f0b1[:, f:f + 1], FIX, ALU.add, ALU.mult)
                last.then_inc(free, 1)
                misc_done(dve, ("h0", b, i))
                link(dve.tensor_scalar(N, A, MAGIC, MAGIC, ALU.add, ALU.subtract))

            def floor(b, i):
                F, N, Cl, J = temps(b)[0:4]
                link(dve.tensor_scalar(Cl, N, -4 * FIX, 4 * FIX - 1, ALU.max, ALU.min))
                link(dve.tensor_scalar(F, Cl, 1.0 / 64, -31.5 / 64, ALU.mult, ALU.add))
                dve.tensor_scalar(J, F, MAGIC, MAGIC, ALU.add, ALU.subtract).then_inc(breaks, 1)
                dve.wait_ge(breaks, 2 * b + i + 1)

            def frac(b, i):
                F, N, Cl, J = temps(b)[0:4]
                link(dve.scalar_tensor_tensor(F, J, -64.0, Cl, ALU.mult, ALU.add))

            def slope(b, i):
                F, N, Cl, J, Y0, Y1 = temps(b)
                dve.wait_ge(nodes, 2 * (2 * b + i + 1))
                link(dve.tensor_tensor(Y1, Y1, Y0, ALU.subtract))
                link(dve.scalar_tensor_tensor(F, F, 4.0, Y1, ALU.mult, ALU.mult))

            def interp(b, i):
                F, N, Cl, J, Y0, Y1 = temps(b)
                link(dve.scalar_tensor_tensor(Y0, Y0, FIX, F, ALU.mult, ALU.add))
                link(dve.tensor_scalar(Y0, Y0, MAGIC, MAGIC + 4 * FIX - 1, ALU.add, ALU.subtract))
                dve.scalar_tensor_tensor(fixed[b // 2][:, 6 + i, :], N, 4 * FIX - 1, Y0, ALU.max, ALU.add).then_inc(hidden, 1)
                dve.wait_ge(hidden, 2 * b + i + 1)

            def add0(b):
                ps, free = misc_wait(dve, ("z0", b))
                flat = ytmp[:, :, :].rearrange("p a b -> p (a b)")
                dve.scalar_tensor_tensor(ytmp[:, :, :], ps[:, 0:T * P].rearrange("p (a b) -> p a b", a=T), 1.0 / FIX,
                                         f0b2[:, :].unsqueeze(1).broadcast_to([P, T, P]), ALU.mult, ALU.add).then_inc(free, 1)
                misc_done(dve, ("z0", b))
                link(dve.tensor_scalar(flat, flat, FIX, MAGIC, ALU.mult, ALU.add))
                link(dve.tensor_scalar(flat, flat, MAGIC, 1.0 / FIX, ALU.subtract, ALU.mult))
                link(dve.tensor_tensor(x_sb[:, b * T:(b + 1) * T, :], x_sb[:, b * T:(b + 1) * T, :], ytmp[:, :, :], ALU.add))

            def keys1(b):
                dve.wait_ge(k_hi, B * M0 + b + 1)
                ps, free = misc_wait(dve, ("k1", b))
                dve.scalar_tensor_tensor(kx[:, 1, 0, :], ps, bk1[:, 0:1], kx[:, 0, 0, :], ALU.add, ALU.subtract).then_inc(free, 1)

            def values1(b):
                ps, free = misc_wait(dve, ("v1", b))
                if b == 0:
                    dve.wait_ge(stack_init, 3)
                for kt in range(KT):
                    last = dve.tensor_tensor(v1[:, b % 2, kt, 0:VW * H1].rearrange("p (h c) -> p h c", c=VW)[:, :, 0:DH1],
                                             ps[:, kt * P:(kt + 1) * P].rearrange("p (h d) -> p h d", h=H1),
                                             bv1[:, :].rearrange("p (h d) -> p h d", h=H1), ALU.add)
                last.then_inc(free, 1)

            def queries1(b):
                dve.wait_ge(q_hi, 2 * B + b + 1)
                ps, free = misc_wait(dve, ("q1", b))
                dve.scalar_tensor_tensor(qx[:, 1, 0, :], ps[:, 0:S], bq1[:, 0:1], qx[:, 0, 0, :], ALU.add, ALU.subtract).then_inc(free, 1)

            def heads_t1(b, i):
                ps, free = misc_wait(dve, ("oT1", b, i))
                cols = ps.rearrange("p (h r) -> p h r", r=32)
                link(dve.reciprocal(rden[:, i, :], cols[:, :, DH1]))
                dve.tensor_tensor(a0[:, i * P:(i + 1) * P].rearrange("p (h d) -> p h d", h=H1), cols[:, :, 0:DH1],
                                  rden[:, i, :].unsqueeze(2).broadcast_to([P, H1, DH1]), ALU.mult).then_inc(free, 1)

            def add1(b):
                for i in range(T):
                    add_to_x(b, i, ("y1", b), f1b2[:, :], i * P, i == T - 1)

            def logits(b):
                ps, free = misc_wait(dve, ("logits", b))
                dve.tensor_copy(lg[:, 0, b * T:(b + 1) * T, :], ps[:, 0:T * E].rearrange("p (t e) -> p t e", t=T)).then_inc(free, 1)
                misc_done(dve, ("logits", b))

            def route(half):
                NT = B * T // 2
                r = slice(half * NT, half * NT + NT)
                logit, dif, ex, prob, picked = (lg[:, i, r, :] for i in range(5))
                top, norm_, inv = (gs[:, i, r] for i in range(3))

                def wide(v):
                    return v.unsqueeze(2).broadcast_to([P, NT, E])

                link(dve.tensor_reduce(top, logit, AX_X, ALU.max))
                dve.tensor_tensor(dif, logit, wide(top), ALU.subtract).then_inc(gate_dif, 1)
                dve.wait_ge(gate_exp, half + 1)
                link(dve.tensor_reduce(norm_, ex, AX_X, ALU.add))
                link(dve.reciprocal(inv, norm_))
                link(dve.tensor_tensor(prob, ex, wide(inv), ALU.mult))
                for i in range(NT):
                    this = prob[:, i, :].unsqueeze(2).broadcast_to([P, E, E])
                    other = prob[:, i, :].unsqueeze(1).broadcast_to([P, E, E])
                    dve.tensor_tensor(cmp_[:, 0, half * NT + i, :, :], other, this, ALU.is_gt)
                    last = dve.tensor_tensor(cmp_[:, 1, half * NT + i, :, :], other, this, ALU.is_equal)
                link(last)
                great, same = (cmp_[:, i, r, :, :].rearrange("p t e f -> p t (e f)") for i in range(2))
                link(dve.tensor_tensor(same, same, tri[:, :, :].rearrange("p e f -> p (e f)").unsqueeze(1).broadcast_to([P, NT, E * E]), ALU.mult))
                link(dve.tensor_tensor(great, great, same, ALU.add))
                link(dve.tensor_reduce(picked, cmp_[:, 0, r, :, :], AX_X, ALU.add))
                link(dve.scalar_tensor_tensor(picked, picked, 1.5, prob, ALU.is_lt, ALU.mult))
                link(dve.tensor_reduce(top, picked, AX_X, ALU.add))
                link(dve.tensor_scalar(norm_, top, 1e-8, None, ALU.add))
                link(dve.reciprocal(inv, norm_))
                link(dve.tensor_tensor(comb[:, r, :], picked, wide(inv), ALU.mult))

            def product(k):
                dve.wait_ge(sg_done, k + 1)
                if k >= 2:
                    dve.wait_ge(hl_done, k - 1)
                dve.tensor_tensor(hp[:, k % 2, :], sg[:, k % 2, :], p_sc[:, k % 2, :], ALU.mult).then_inc(hp_done, 1)

            def low(k):
                n, f = k // FF, k % FF
                dve.wait_ge(hh_done, k + 1)
                dve.tensor_tensor(hh[:, n % 2, 1, f, :], hp[:, k % 2, :], hh[:, n % 2, 0, f, :], ALU.subtract).then_inc(hl_done, 1)

            def mix(n):
                half, e = n // E, n % E
                dve.wait_ge(y_full, n + 1)
                if n:
                    dve.wait_ge(y_free, n)
                for i in range(4):
                    tt = half * 4 + i
                    last = dve.scalar_tensor_tensor(x_sb[:, tt, :], p_o[:, n % 2, i * P:(i + 1) * P], comb[:, tt, e:e + 1],
                                                    x_sb[:, tt, :], ALU.mult, ALU.add)
                last.then_inc(y_free, 1)

            def activate(n, f):
                k = n * FF + f
                if n < 2 * E:
                    product(k)
                if k:
                    low(k - 1)
                if f == 3 and n:
                    mix(n - 1)

            dve.memset(kB[SEL0:P, :, :, :].rearrange("p b h k -> p (b h k)").bitcast(F32), 0.0)
            dve.memset(qB[SEL0:P, :, :, :].rearrange("p b h k -> p (b h k)").bitcast(F32), 0.0).then_inc(zero_kb, 1)
            steps = {"ln": norm, "xT": xt, "k0": keys0, "q0": queries0, "max": maxima, "rows": rows, "sT": sums_t, "oT": heads_t,
                     "y0": project0, "up0": fix, "floor": floor, "frac": frac, "slope": slope, "interp": interp, "down0": add0,
                     "k1": keys1, "v1": values1, "q1": queries1, "oT1": heads_t1, "y1": add1, "logits": logits, "route": route,
                     "act": activate, "mix": mix}
            for kind, *at in order:
                if kind in steps:
                    steps[kind](*at)

        @block.scalar
        def _(act):
            def copy_out(dst, key, src=lambda ps: ps):
                ps, free = misc_wait(act, key)
                act.copy(dst, src(ps)).then_inc(free, 1)

            def context(b):
                copy_out(cT[:, b * C:(b + 1) * C], ("cT", b), lambda ps: ps[0:CD, :])

            def keys0(b, m):
                if b and m == 0:
                    act.wait_ge(k_stacked, 96 * b)
                ps, _free = misc_wait(act, ("k0", b, m))
                act.copy(kx[:, 0, m, :], ps).then_inc(k_hi, 1)

            def values0(b, kt):
                copy_out(v0[:, b % 2, kt, :], ("v0", b, kt))

            def xt(n):
                if n < ln_exp(0):
                    copy_out(xT[:, n % 2, :], ("xT", n), lambda ps: ps[:, 0:S])
                else:
                    b = n - ln_exp(0)
                    ps, _free = misc_wait(act, ("xT", n))
                    act.copy(xT[:, n % 2, :], ps[:, 0:S])
                    act.copy(xh[:, 0, b * S:(b + 1) * S], ps[:, 0:S]).then_inc(xh_hi, 1)

            def queries0(b, i):
                if b and i == 0:
                    act.wait_ge(q_stacked, 96 * b)
                ps, _free = misc_wait(act, ("q0", b, i))
                act.copy(qx[:, 0, 2 * i:2 * i + 2, :].rearrange("p m n -> p (m n)"), ps).then_inc(q_hi, 1)

            def softmax(layer, b, h):
                u = head_number(layer, b, h)
                n = group_number(layer, b, h // 4)
                for half in range(2):
                    act.wait_ge(sc_full[half], u + 1)
                    if half == 0 and n > 1:
                        act.wait_ge(av_done, n - 1)
                    act.activation(probs[:, h % 8, half * 512:(half + 1) * 512], p_sc[:, half, :], ACT.Exp,
                                   scale=(DH0 if layer == 0 else DH1) ** -0.5).then_inc(sc_free[half], 1)

            def outputs(layer, b, g, c):
                if c < 3:
                    return
                n = group_number(layer, b, g)
                act.wait_ge(av_done, n + 1)
                if layer == 0:
                    act.copy(osb[:, 2 * g:2 * g + 2, :].rearrange("p m n -> p (m n)"), p_o[:, 0, :])
                    act.copy(ssb[:, g, :], p_o[:, 1, 0:S]).then_inc(o_free, 1)
                else:
                    act.copy(osb[:, g, :], p_o[:, n % 2, 0:S]).then_inc(o_free, 1)

            def heads_back(b, i):
                copy_out(aT[:, :], ("aT", b, i))

            def nodes_at(b, i):
                J, Y0, Y1 = (fixed[b // 2][:, j, :] for j in (3, 4, 5))
                act.wait_ge(breaks, 2 * b + i + 1)
                act.activation(Y0, J, ACT.Gelu, scale=0.25).then_inc(nodes, 1)
                act.activation(Y1, J, ACT.Gelu, bias=quarter[:, 0:1], scale=0.25).then_inc(nodes, 1)

            def keys1(b):
                act.wait_ge(k_stacked, 96 * B + 48 * b)
                ps, _free = misc_wait(act, ("k1", b))
                act.activation(kx[:, 0, 0, :], ps, ACT.Identity, bias=bk1[:, 0:1]).then_inc(k_hi, 1)

            def queries1(b):
                act.wait_ge(q_stacked, 96 * B + 48 * b)
                ps, _free = misc_wait(act, ("q1", b))
                act.activation(qx[:, 0, 0, :], ps[:, 0:S], ACT.Identity, bias=bq1[:, 0:1]).then_inc(q_hi, 1)

            def heads_back1(b):
                copy_out(aT[:, 0:S], ("aT1", b), lambda ps: ps[:, 0:S])

            def up1(b):
                ps, free = misc_wait(act, ("h1", b))
                act.activation(ssb[:, 0, :], ps[:, 0:S], ACT.Relu, bias=f1b1[:, 0:1])
                act.activation(ssb[:, 1, :], ps[:, S:2 * S], ACT.Relu, bias=f1b1[:, 1:2]).then_inc(free, 1)

            def route(half):
                NT = B * T // 2
                act.wait_ge(gate_dif, half + 1)
                act.activation(lg[:, 2, half * NT:(half + 1) * NT, :], lg[:, 1, half * NT:(half + 1) * NT, :], ACT.Exp).then_inc(gate_exp, 1)

            def activate(n, f):
                k = n * FF + f
                if n < 2 * E:
                    if k == 0:
                        act.wait_ge(av_done, 6 * B)
                    act.wait_ge(gu_full, k + 1)
                    act.activation(sg[:, k % 2, :], p_max[:, k % 2, :], ACT.Silu).then_inc(sg_done, 1)
                if k:
                    last_n, last_f = (k - 1) // FF, (k - 1) % FF
                    act.wait_ge(hp_done, k)
                    if last_n >= 2 and last_f == 0:
                        act.wait_ge(y_full, last_n - 1)
                    act.copy(hh[:, last_n % 2, 0, last_f, :], hp[:, (k - 1) % 2, :]).then_inc(hh_done, 1)

            steps = {"cT": context, "k0": keys0, "v0": values0, "xT": xt, "q0": queries0, "sc": softmax, "av": outputs,
                     "aT": heads_back, "nodes": nodes_at, "k1": keys1, "q1": queries1, "aT1": heads_back1, "h1": up1,
                     "route": route, "act": activate}
            for kind, *at in order:
                if kind in steps:
                    steps[kind](*at)

        @block.gpsimd
        def _(pool):
            chain = [0]

            def link(ins):
                chain[0] += 1
                ins.then_inc(pool_chain, 1)
                pool.wait_ge(pool_chain, chain[0])

            def norm(n):
                pool.wait_ge(ln_var, n + 1)
                link(pool.tensor_scalar(veps[:, n % 2, :], meanvar[:, n % 2, :, 1], EPS, None, ALU.add))
                pool.tensor_tensor(rstd[:, n % 2, :], veps[:, n % 2, :], mhalf[:, :], ALU.pow).then_inc(ln_rstd, 1)
                pool.wait_ge(ln_rstd, n + 1)

            def stacks1(b):
                link(pool.memset(kS[:, b, :, :].rearrange("p h k -> p (h k)").bitcast(F32), 0.0))
                link(pool.affine_select(out=kS[SEL1:P, b, :, :], in_=kS[SEL1:P, b, :, :], compare_op=ALU.not_equal,
                                        fill=-1.0, base=0, pattern=[[-1, H1], [0, C]], channel_multiplier=1))

            def init(n):
                if n == 0:
                    pool.wait_ge(zero_kb, 1)
                    for b in range(2):
                        link(pool.affine_select(out=kB[SEL0:P, b, :, :], in_=kB[SEL0:P, b, :, :], compare_op=ALU.not_equal,
                                                fill=-1.0, base=0, pattern=[[-1, H0], [0, C]], channel_multiplier=1))
                elif n == 1:
                    for b in range(2):
                        link(pool.memset(qS[:, b, :, :].rearrange("p h k -> p (h k)").bitcast(F32), 0.0))
                    link(pool.memset(tri[:, :, :], 1.0))
                    link(pool.affine_select(out=tri[:, :, :], in_=tri[:, :, :], compare_op=ALU.is_gt, fill=0.0, base=0,
                                            pattern=[[1, E], [-1, E]], channel_multiplier=0))
                    stacks1(0)
                elif n == 2:
                    pool.wait_ge(av_done, 2 * (B - 1))
                    link(pool.memset(v1, 0.0))
                    for b in range(2):
                        link(pool.memset(v1[:, b, :, 0:VW * H1].rearrange("p k (h c) -> p k h c", c=VW)[:, :, :, DH1], 1.0))
                else:
                    misc_done(pool, ("z0", 1))
                    stacks1(1)
                pool.sem_inc(stack_init, 1)

            def sums(b, h):
                u = head_number(0, b, h)
                n = group_number(0, b, h // 4)
                pool.wait_ge(sc_free[0], u + 1)
                pool.wait_ge(sc_free[1], u + 1)
                if n and h % 4 == 0:
                    pool.wait_ge(av_done, n)
                tiles = [probs[:, h % 8, kt * S:(kt + 1) * S] for kt in range(KT)]
                link(pool.tensor_tensor(psums[:, h % 4, :], tiles[0], tiles[1], ALU.add))
                link(pool.tensor_tensor(psums[:, h % 4, :], psums[:, h % 4, :], tiles[2], ALU.add))
                pool.tensor_tensor(psums[:, h % 4, :], psums[:, h % 4, :], tiles[3], ALU.add).then_inc(sums_set, 1)
                pool.wait_ge(sums_set, u + 1)

            def split(c):
                w, e = (c % 2, c // 2) if c < 2 * E else (2, c - 2 * E)
                pool.wait_ge(ld_stage[c % 2], 16 * (c // 2 + 1))
                link(pool.tensor_copy(ew[w][:, 0, e, :], stage[:, c % 2, :]))
                pool.tensor_tensor(ew[w][:, 1, e, :], stage[:, c % 2, :], ew[w][:, 0, e, :], ALU.subtract).then_inc(stage_free, 1)
                pool.wait_ge(stage_free, c + 1)

            link(pool.memset(ident[:, :], 0.0))
            link(pool.affine_select(out=ident[:, :], in_=ident[:, :], compare_op=ALU.not_equal, fill=1.0, base=0,
                                    pattern=[[-1, P]], channel_multiplier=1))
            pool.sem_inc(const_pe, 1)
            link(pool.memset(mhalf[:, :], -0.5))
            link(pool.memset(quarter[:, :], 0.25))
            link(pool.memset(ones[:, :], 1.0))
            pool.sem_inc(const_pe, 1)
            steps = {"ln": norm, "sum": sums, "init": init, "split": split}
            for kind, *at in order:
                if kind in steps:
                    steps[kind](*at)

        @block.sync
        def _(sp):
            def row(v):
                return v.rearrange("(a d) -> a d", a=1).partition_broadcast(P)

            sp.dma_start(raw, t["ctx_768"].rearrange("b (k p) d -> p (b k) d", p=P)).then_inc(ld_c, 16)
            sp.dma_start(x_sb[:, :, :], t["x"].rearrange("b (i p) d -> p (b i) d", p=P)).then_inc(ld_x, 16)
            for dst, src in ((wk0, "L0_xattn_Wk"), (wv0, "L0_xattn_Wv"), (wq0, "L0_xattn_Wq")):
                sp.dma_start(dst[:, :], t[src]).then_inc(ld_w0, 16)

            def stack0(b):
                for src, what, landed, a, bb in ((kx, "k0", k_stacked, kA, kB), (qx, "q0", q_stacked, qA, qB)):
                    for i in range(M0 if what == "k0" else 2):
                        misc_done(sp, (what, b, i))
                    if b >= 2:
                        sp.wait_ge(sc_full[1], head_number(0, b - 1, 0))
                    for i in range(2):
                        rows = slice(64 * i, 64 * i + 64)
                        low = 0 if what == "k0" else 1
                        sp.dma_start(a[0:64, b % 2, i::2, :], src[rows, 0, :, :]).then_inc(landed, 16)
                        sp.dma_start(a[64:128, b % 2, i::2, :], src[rows, low, :, :]).then_inc(landed, 16)
                        sp.dma_start(bb[0:64, b % 2, i::2, :], src[rows, 1 - low, :, :]).then_inc(landed, 16)

            def stack1(b):
                for src, key, bounced, scr, dst, landed, parts in (
                        (kx, "k1", k_bounced, dk, kS, k_stacked, (0, 1, 0)), (qx, "q1", q_bounced, dq, qS, q_stacked, (0, 0, 1))):
                    misc_done(sp, (key, b))
                    sp.dma_start(scr[b], src[:, :, 0, :]).then_inc(bounced, 16)
                for src, key, bounced, scr, dst, landed, parts in (
                        (kx, "k1", k_bounced, dk, kS, k_stacked, (0, 1, 0)), (qx, "q1", q_bounced, dq, qS, q_stacked, (0, 0, 1))):
                    sp.wait_ge(bounced, 16 * (b + 1))
                    if key == "k1":
                        sp.wait_ge(stack_init, 2 if b == 0 else 4)
                        if b >= 2:
                            sp.wait_ge(sc_full[1], head_number(1, b - 1, 0))
                    view = scr[b].rearrange("(h d) s n -> s d h n", d=DH1)
                    for i, part in enumerate(parts):
                        sp.dma_start(dst[DH1 * i:DH1 * (i + 1), b % 2, :, :], view[part]).then_inc(landed, 16)

            experts = [t["L1_ffn_W1"], t["L1_ffn_W3"], t["L1_ffn_W2"].rearrange("e (f p) d -> e p f d", p=P)]

            def stage_in(c):
                w, e = (c % 2, c // 2) if c < 2 * E else (2, c - 2 * E)
                if c == 0:
                    sp.wait_ge(av_done, 2 * B)
                if c == 2 * E:
                    misc_done(sp, ("z0", B - 1))
                if c >= 2:
                    sp.wait_ge(stage_free, c - 1)
                dst = stage[:, c % 2, :]
                if w == 2:
                    dst = dst.rearrange("p (f d) -> p f d", f=FF)
                sp.dma_start(dst, experts[w][e]).then_inc(ld_stage[c % 2], 16)

            def rest_of_weights(n):
                if n != 1:
                    return
                sp.dma_start(wo0[:, :, :], t["L0_xattn_Wo"].rearrange("(m p) n -> p m n", p=P)).then_inc(ld_w1, 16)
                sp.dma_start(f0w1[:, :], t["L0_ffn_w1"]).then_inc(ld_w1, 16)
                sp.dma_start(f0w2[:, :, :], t["L0_ffn_w2"].rearrange("(m p) n -> p m n", p=P)).then_inc(ld_w1, 16)
                sp.dma_start(f0b1[:, :], t["L0_ffn_b1"]).then_inc(ld_w1, 16)
                sp.dma_start(bo0[:, :], row(t["L0_xattn_bo"])).then_inc(ld_w1, 16)
                sp.dma_start(f0b2[:, :], row(t["L0_ffn_b2"])).then_inc(ld_w1, 16)
                for dst, src in ((wq1, "L1_xattn_Wq"), (wk1, "L1_xattn_Wk"), (wv1, "L1_xattn_Wv"), (f1w1, "L1_xattn_W1"),
                                 (wg, "L1_ffn_Wg"), (f1b1, "L1_xattn_b1"), (bq1, "L1_xattn_bq"), (bk1, "L1_xattn_bk")):
                    sp.dma_start(dst[:, :], t[src]).then_inc(ld_w2, 16)
                sp.dma_start(f1w2[:, :, :], t["L1_xattn_W2"].rearrange("(m p) n -> p m n", p=P)).then_inc(ld_w2, 16)
                sp.dma_start(bv1[:, :], row(t["L1_xattn_bv"])).then_inc(ld_w2, 16)
                sp.dma_start(f1b2[:, :], row(t["L1_xattn_b2"])).then_inc(ld_w2, 16)

            steps = {"stack0": stack0, "stack1": stack1, "stage": stage_in, "init": rest_of_weights}
            for kind, *at in order:
                if kind in steps:
                    steps[kind](*at)
            for half in range(2):
                sp.wait_ge(y_free, E * (half + 1))
                sp.dma_start(out.rearrange("b (i p) d -> p (b i) d", p=P)[:, half * 4:half * 4 + 4, :],
                             x_sb[:, half * 4:half * 4 + 4, :]).then_inc(stored, 16)
            sp.wait_ge(stored, 32)


_INS = ['x', 'ctx_768', 'L0_xattn_Wq', 'L0_xattn_Wk', 'L0_xattn_Wv', 'L0_xattn_Wo', 'L0_xattn_bo', 'L0_ffn_w1', 'L0_ffn_b1',
        'L0_ffn_w2', 'L0_ffn_b2', 'L1_xattn_Wq', 'L1_xattn_bq', 'L1_xattn_Wk', 'L1_xattn_bk', 'L1_xattn_Wv', 'L1_xattn_bv',
        'L1_xattn_W1', 'L1_xattn_b1', 'L1_xattn_W2', 'L1_xattn_b2', 'L1_ffn_Wg', 'L1_ffn_W1', 'L1_ffn_W2', 'L1_ffn_W3']


def kernel(**inputs):
    import numpy as _np
    import concourse.bacc as _bacc
    from concourse import mybir as _mybir
    from concourse.bass_utils import run_bass_kernel_spmd as _run

    nc = _bacc.Bacc("TRN2", target_bir_lowering=False, num_devices=1)
    arrays, aps = {}, {}
    for name in _INS:
        a = _np.asarray(inputs[name])
        if name in ("L0_ffn_b1", "L1_xattn_b1", "L1_xattn_bq", "L1_xattn_bk"):
            a = a.reshape(-1, P).T
        a = _np.ascontiguousarray(a)
        arrays[f"in_{name}_dram"] = a
        aps[name] = nc.dram_tensor(f"in_{name}_dram", a.shape, _mybir.dt.from_np(a.dtype), kind="ExternalInput").ap()
    out = nc.dram_tensor("out_dram", (B, S, P), _mybir.dt.float32, kind="ExternalOutput").ap()
    build(nc, aps, out)
    r = _run(nc, [arrays], core_ids=[0])
    return r.results[0]["out_dram"]
```

```python
from contextlib import ExitStack

import concourse.bass as bass
from concourse import mybir

ALU = mybir.AluOpType
ACT = mybir.ActivationFunctionType
F32 = mybir.dt.float32
F16 = mybir.dt.float16
AX_X = mybir.AxisListType.X

P = 128
B = 4
S = 256
T = 2
C = 512
CD = 96
KT = C // P
H0, DH0 = 8, 64
H1, DH1 = 16, 8
M0 = H0 * DH0 // P
FF = 4
E = 8
MAGIC = 12582912.0
FIX = 256.0
STEP = 64
BREAK = STEP * MAGIC
EPS = 1e-5
SEL0 = 64
SEL1 = 96
VW = DH1 + 1


PLACES = {
    0: {"max": (1.5, 1.0), "sum": 1.38, "av": (-0.38, 0.96), "f_ln": -0.65, "f_xn": 0.92, "f_xT": 1.2,
        "up0": (1.4, 0.13), "round": 1.57, "floor": 2.0, "nodes": 2.17, "slope": 3.0, "interp": 3.5, "ident": 3.7,
        "down0": 4.26, "q1_ln": 4.45, "q1_xn": 4.74, "q1_xT": 5.3, "q1": 6.29, "k1": 2.03, "bounce": 5.87,
        "sT": 4.02, "oT": (5.14, 0.74), "aT": (5.76, 0.9), "y0": (6.08, 1.12), "v0": (3.6, 1.0),
        "k0": (2.01, 0.41), "q0_ln": -0.27, "q0_xn": 1.32, "q0_xT": 1.04, "q0": (1.92, 0.5), "v1": 5.11,
        "zeros": 3.67, "init": (1.0, 2.0), "rows": 0.84},
    1: {"max": (2.4, 1.01), "av": (0.3, 1.0), "f_ln": 0.18, "f_xn": 1.29, "f_xT": 1.39, "up0": (1.87, 0.4),
        "round": 2.76, "floor": 2.8, "nodes": 3.39, "slope": 4.4, "interp": 5.2, "ident": 5.69, "down0": 5.86,
        "q1_ln": 8.4, "q1_xn": 9.17, "q1_xT": 10.0, "q1": 11, "k1": 9.53, "bounce": 11.61, "sT": 4.1,
        "oT": (4.64, 2.0), "aT": (6.0, 2.0), "y0": (7.3, 2.0), "oT1": (4.52, 0.7), "aT1": 6.54, "h1": 8.28,
        "y1": 9.07, "v1": 5.94, "stage": (0.62, 1.9), "split": (0.6, 1.9), "ex_ln": (11.14, 1.0),
        "ex_xn": (12.57, 1.0), "ex_xT": (12.68, 1.0), "logits": (14.14, 1.0), "route": 16.14, "rows": 2.43},
}

SHIFTED = {
    (0, 'init'): (0.81, 2.0), (0, 'k0'): (3.3, 0.6), (0, 'max'): (3.9, 0.65), (0, 'q0'): (6.4, 0.5),
    (0, 'q0_xT'): 5.8, (0, 'q0_xn'): 5.08, (0, 'rows'): 0.26, (0, 'v0'): (7.61, 0.7), (1, 'av'): (-0.19, 1.0),
    (1, 'k0'): (2.01, 0.61), (1, 'max'): (1.87, 1.0), (1, 'q0'): (1.33, 0.5), (2, 'down0'): 4.35,
    (2, 'f_ln'): 0.02, (2, 'interp'): 3.48, (2, 'q1'): 5.66, (2, 'slope'): 2.71, (2, 'sum'): 2.35,
    (2, 'v0'): (3.6, 1.02), (3, 'av'): (-0.45, 0.96), (3, 'nodes'): 2.58, (3, 'oT'): (5.14, 0.71), (3, 'sT'): 3.68,
    (3, 'v1'): 5.23, (4, 'av'): (0.05, 1.0), (4, 'bounce'): 12.04, (4, 'down0'): 7.55, (4, 'f_ln'): 1.46,
    (4, 'f_xT'): 2.5, (4, 'f_xn'): 2.1, (4, 'floor'): 3.9, (4, 'ident'): 6.9, (4, 'interp'): 6.3,
    (4, 'nodes'): 4.19, (4, 'oT'): (5.0, 1.99), (4, 'round'): 3.55, (4, 'rows'): 2.08, (4, 'slope'): 5.5,
    (4, 'up0'): (2.97, 0.4), (5, 'down0'): 6.46, (5, 'f_xT'): 1.72, (5, 'oT1'): (4.69, 0.7),
    (5, 'split'): (-0.81, 1.9), (5, 'stage'): (0.5, 2.08), (5, 'y1'): 8.94, (6, 'aT1'): 6.21, (6, 'h1'): 7.87,
    (6, 'max'): (2.62, 1.01), (6, 'oT1'): (4.19, 0.7), (6, 'y1'): 8.74, (7, 'ex_ln'): (11.42, 1.0)}


def schedule():
    placed = []

    def put(it, place, *step):
        heads = H0 if it < B else H1
        if place >= heads:
            it, place = it + 1, place - heads
        placed.append((it, place, len(placed), step))

    first = [("init", 0), ("warm", 10), ("ln", "q0", 0), ("split_w", 0), ("cT", 0), ("warm", 6), ("xn", "q0", 0), ("k0", 0, 0), ("warm", 4), ("xT", "q0", 0), ("k0", 0, 1), ("k0", 0, 2), ("k0", 0, 3),
             ("q0", 0, 0), ("q0", 0, 1), ("stack0", 0), ("split_w", 1), ("cT", 1), ("ln", "q0", 1), ("v0", 0, 0), ("v0", 0, 1), ("xn", "q0", 1), ("init", 1),
             ("v0", 0, 2), ("v0", 0, 3), ("cT", 2), ("cT", 3), ("xT", "q0", 1),
             ("max", 0, 0, 0), ("k0", 1, 0), ("max", 0, 0, 1), ("k0", 1, 1), ("max", 0, 0, 2), ("k0", 1, 2), ("max", 0, 0, 3), ("rows", 0, 0, 0)]
    for what in first:
        put(-1, 0, *what)
    for n, h in enumerate(range(4, H0)):
        put(0, 0.5 + 0.6 * n, "max", 0, 0, h)
    put(0, 3.1, "rows", 0, 0, 1)
    put(0, 0.1, "k0", 1, 3)
    for i in range(2):
        put(0, 0.7 + 0.6 * i, "q0", 1, i)

    for it in range(2 * B):
        layer, b = it // B, it % B
        heads = H0 if layer == 0 else H1
        at = PLACES[layer]

        def step(name, *what, n=0):
            place = SHIFTED.get((it, name), at[name])
            put(it, place if not isinstance(place, tuple) else place[0] + n * place[1], *what)

        nxt = (layer, b + 1) if b + 1 < B else (1, 0) if layer == 0 else None
        if nxt:
            put(it, 1.7 if it == 0 else -0.01, "stack0" if nxt[0] == 0 else "stack1", nxt[1])
            for h in range(H0 if nxt[0] == 0 else H1):
                n = h if (nxt[0] == layer) else h / 2
                step("max", "max", *nxt, h, n=n)
                if h % 4 == 3:
                    first_max, distance = SHIFTED.get((it, "max"), at["max"])
                    put(it, first_max + n * distance + SHIFTED.get((it, "rows"), at["rows"]), "rows", *nxt, h // 4)
        for h in range(heads):
            put(it, h, "sc", layer, b, h)
            if layer == 0:
                put(it, h + SHIFTED.get((it, "sum"), at["sum"]), "sum", b, h)
        for g in range(heads // 4):
            first_chunk, distance = SHIFTED.get((it, "av"), at["av"])
            for c in range(4):
                put(it, 4 * g + 4 + first_chunk + c * distance, "av", layer, b, g, c)

        if 1 <= it <= B:
            step("sT", "sT", it - 1)
            for i in range(T):
                for name in ("oT", "aT", "y0"):
                    step(name, name, it - 1, i, n=i)
        if 2 <= it <= B + 1:
            f = it - 2
            step("f_ln", "ln", "f", f)
            step("f_xn", "xn", "f", f)
            step("f_xT", "xT", "f", f)
            for i in range(2):
                step("up0", "up0", f, i, n=i)
            for name in ("round", "floor", "nodes", "slope", "interp", "ident", "down0"):
                step(name, name, f)
            step("k1", "k1", f)
            step("q1_ln", "ln", "q1", f)
            step("q1_xn", "xn", "q1", f)
            step("q1_xT", "xT", "q1", f)
            step("q1", "q1", f)
            step("bounce", "bounce", f)
        if it == 0:
            for i in range(2, 5):
                step("init", "init", i, n=i - 2)
        if it < B - 1:
            for kt in range(KT):
                step("v0", "v0", b + 1, kt, n=kt)
        if it < B - 2:
            for m in range(M0):
                step("k0", "k0", b + 2, m, n=m)
            step("q0_ln", "ln", "q0", b + 2)
            step("q0_xn", "xn", "q0", b + 2)
            step("q0_xT", "xT", "q0", b + 2)
            for i in range(2):
                step("q0", "q0", b + 2, i, n=i)
        if B - 1 <= it < 2 * B - 1:
            if it == B - 1:
                step("v1", "init", 5)
                step("zeros", "zeros")
            step("v1", "v1", it - B + 1)
        if it > B:
            project1(lambda name, n, *what: step(name, *what, n=n), b - 1)
        if B <= it < 2 * B - 1:
            for i in range(8):
                c = 8 * b + i
                step("stage", "stage", c, n=i)
                if c:
                    step("split", "split", c - 1, n=i)
        if it == 2 * B - 1:
            put(it, 0, "split", 3 * E - 1)
            for i in range(2):
                tokens(lambda name, n, *what: step(name, *what, n=n), i, i)
            step("route", "route", 0)
    order = [what for _, _, _, what in sorted(placed)]

    rest = {0: [("oT1", B - 1, 0)], 1: [("oT1", B - 1, 1)], 2: [("shares", 0)], 3: [("compare", 0)], 4: [("rank", 0)], 5: [("best", 0)],
            6: [("aT1", B - 1)], 8: [("h1", B - 1)], 10: [("y1", B - 1)]}
    for i, b in enumerate((2, 3)):
        for chunk, kind in ((11, "ln"), (13, "xn"), (15, "xT")):
            rest[chunk + 5 * i] = rest.get(chunk + 5 * i, []) + [(kind, "ex", b)]
        rest[17 + 5 * i] = [("logits", b)]
    rest.update({24: [("route", 1)], 28: [("shares", 1)], 30: [("compare", 1)], 34: [("rank", 1)], 36: [("best", 1)]})
    for n in range(2 * E):
        for f in range(FF):
            order.append(("gu", n, f))
            if n and f >= 2:
                order.extend([("dn", n - 1, 2 * (f - 2)), ("dn", n - 1, 2 * (f - 2) + 1)])
            order.append(("act", n, f))
            order.extend(rest.get(FF * n + f, []))
    order += [("dn_last", f) for f in range(FF - 1)] + [("act", 2 * E, 0), ("dn_last", FF - 1), ("mix", 2 * E - 1)]

    for b in range(B):
        turn = [("y0", b, 1), ("ln", "f", b), ("xn", "f", b), ("xT", "f", b), ("up0", b, 0), ("up0", b, 1), ("round", b), ("floor", b),
                ("nodes", b), ("slope", b), ("interp", b), ("ident", b), ("down0", b), ("ln", "q1", b), ("xn", "q1", b),
                ("xT", "q1", b), ("q1", b), ("y1", b), ("ln", "ex", b), ("xn", "ex", b), ("xT", "ex", b), ("logits", b)]
        at = [order.index(what) for what in turn]
        assert at == sorted(at), turn
    return order


def project1(put, b):
    for i in range(T):
        put("oT1", i, "oT1", b, i)
    put("aT1", 0, "aT1", b)
    put("h1", 0, "h1", b)
    put("y1", 0, "y1", b)


def tokens(put, b, n):
    put("ex_ln", n, "ln", "ex", b)
    put("ex_xn", n, "xn", "ex", b)
    put("ex_xT", n, "xT", "ex", b)
    put("logits", n, "logits", b)


def build(nc, t, out):
    ctx = ExitStack()
    with ctx:
        def sb(name, shape, dt=F32):
            return ctx.enter_context(nc.sbuf_tensor(name, shape, dt))

        def sem(name):
            return ctx.enter_context(nc.semaphore(name))

        def sems(name, n):
            return [sem(f"{name}{i}") for i in range(n)]

        ident = sb("ident", [P, P])
        x_sb = sb("x_sb", [P, B * T, P])
        cT = sb("cT", [CD, 2, B * C], F16)
        wc = sb("wc", [CD, 2, 2 * H0 * DH0 + 2 * P], F16)
        wq0 = sb("wq0", [P, H0 * DH0])
        wo0 = sb("wo0", [P, M0, P])
        f0w1 = sb("f0w1", [P, FF * P])
        f0w2 = sb("f0w2", [P, FF, P])
        f0b1 = sb("f0b1", [P, FF])
        f0b1x = sb("f0b1x", [P, FF])
        wq1 = sb("wq1", [P, P])
        bq1 = sb("bq1", [P, 1])
        bk1 = sb("bk1", [P, 1])
        f1w1 = sb("f1w1", [P, 2 * P])
        f1w2 = sb("f1w2", [P, 2, P])
        f1b1 = sb("f1b1", [P, 2])
        wg = sb("wg", [P, E])
        bo0 = sb("bo0", [P, P])
        f0b2 = sb("f0b2", [P, P])
        bv1 = sb("bv1", [P, P])
        f1b2 = sb("f1b2", [P, P])
        region = sb("region", [P, 24576], F16)
        kA = region[:, 0:8192].rearrange("p (b h k) -> p b h k", b=2, h=H0)
        kB = region[:, 8192:16384].rearrange("p (b h k) -> p b h k", b=2, h=H0)
        qA = region[:, 16384:20480].rearrange("p (b h k) -> p b h k", b=2, h=H0)
        qB = region[:, 20480:24576].rearrange("p (b h k) -> p b h k", b=2, h=H0)
        ew = [region[:, 8192 * i:8192 * (i + 1)].rearrange("p (s e n) -> p s e n", s=2, e=E) for i in range(3)]
        kS = sb("kS", [P, 2, H1, C], F16)
        qS = sb("qS", [P, 2, H1, S], F16)
        kx = sb("kx", [P, 2, M0, C], F16)
        qx = sb("qx", [P, 2, M0, S], F16)
        v0 = sb("v0", [P, 2, KT, H0 * DH0])
        VR = VW * H1 + 32 - VW
        v1 = v0[:, 0, :, :].rearrange("p k n -> p (k n)")[:, 0:2 * KT * VR].rearrange("p (b k n) -> p b k n", b=2, k=KT)
        stage = v0[:, 1, 0:2, :]
        probs = sb("probs", [P, 8, KT * S])
        raw = probs[:, 0:2, :].rearrange("p a b -> p (a b)")[:, 0:B * KT * CD].rearrange("p (c d) -> p c d", d=CD)
        wc_in = probs[0:CD, 2:4, :].rearrange("p a b -> p (a b)")[:, 0:2 * H0 * DH0 + 2 * P]
        xn = sb("xn", [P, 2, T, P])
        xT = sb("xT", [P, 2, S])
        xh = qS[:, 0, 0:8, :].rearrange("p h n -> p (h n)").rearrange("p (s n) -> p s n", s=2)
        cmp_ = kS[:, 0, 0:4, :].rearrange("p h n -> p (h n)").bitcast(F32).rearrange("p (s t e f) -> p s t e f", s=2, t=B * T, e=E)
        mx = sb("mx", [P, 2, T, H1])
        stats = sb("stats", [P, T, 6])
        meanvar = sb("meanvar", [P, 2, T, 2])
        veps = sb("veps", [P, 2, T])
        rstd = sb("rstd", [P, 2, T])
        mhalf = sb("mhalf", [P, T])
        euler = sb("euler", [P, 1])
        ones = sb("ones", [P, 32])
        node_bias = sb("node_bias", [P, 2])
        osb = sb("osb", [P, 4, S])
        ssb = sb("ssb", [P, 2, S])
        rden = sb("rden", [P, T, H1])
        a0 = sb("a0", [P, M0 * P])
        aT = sb("aT", [P, M0 * P])
        ytmp = sb("ytmp", [P, T, P])
        lg = kS[:, 0, 4:6, :].rearrange("p h n -> p (h n)").bitcast(F32).rearrange("p (i t e) -> p i t e", i=8, t=B * T)
        gs = sb("gs", [P, 4, B * T])
        tri = sb("tri", [P, E, E])
        comb = sb("comb", [P, B * T, E])
        fixed = [v.rearrange("p (i n) -> p i n", n=FF * S) for v in (
            kS[:, 1, :, :].rearrange("p h n -> p (h n)").bitcast(F32), region[:, 16384:24576].bitcast(F32))]
        warm_in = qx[:, 0, 0:2, :].rearrange("p m n -> p (m n)")
        psums = sb("psums", [P, 4, S])
        mrow = sb("mrow", [4, S], F16)
        sg = probs[:, 0, :].rearrange("p (a b) -> p a b", a=2)
        hp = probs[:, 1, :].rearrange("p (a b) -> p a b", a=2)
        hh = probs[:, 2:6, :].bitcast(F16).rearrange("p (b s) (f n) -> p b s f n", b=2, f=FF)

        p_sc = ctx.enter_context(nc.psum_tensor("p_sc", [P, 2, 512], F32))
        p_o = ctx.enter_context(nc.psum_tensor("p_o", [P, 2, 512], F32))
        p_misc = ctx.enter_context(nc.psum_tensor("p_misc", [P, 4, 512], F32))

        dk = nc.dram_tensor("k_scratch", (B, P, 2, C), F16).ap()
        dq = nc.dram_tensor("q_scratch", (B, P, 2, S), F16).ap()

        ld_x, ld_c = sems("ld_x", 2), sems("ld_c", 2)
        ld_wk0, ld_w0, ld_wc, ld_w1, ld_w2 = (sem(f"ld_{n}") for n in ("wk0", "w0", "wc", "w1", "w2"))
        wc_hi, wc_split, c_hi = sem("wc_hi"), sem("wc_split"), sem("c_hi")
        ld_stage = sems("ld_stage", 2)
        stage_free = sem("stage_free")
        stack_copied = sem("stack_copied")
        warm_set = sem("warm_set")
        const_pe, zero_kb, stack_init = sem("const_pe"), sem("zero_kb"), sem("stack_init")
        misc_full = sems("misc_full", 4)
        misc_free = sems("misc_free", 4)
        ln_var, ln_rstd, ln_xn = sem("ln_var"), sem("ln_rstd"), sem("ln_xn")
        k_hi, q_hi = sem("k_hi"), sem("q_hi")
        k_stacked, q_stacked = sem("k_stacked"), sem("q_stacked")
        k_bounced, q_bounced = sem("k_bounced"), sem("q_bounced")
        rows_set = sem("rows_set")
        sc_full, sc_free = sems("sc_full", 2), sems("sc_free", 2)
        sums_set = sem("sums_set")
        av_done, o_free = sem("av_done"), sem("o_free")
        f0b1_set, breaks, nodes, hidden = sem("f0b1_set"), sem("breaks"), sem("nodes"), sem("hidden")
        logits_set, gate_dif, gate_exp, xh_hi = sem("logits_set"), sem("gate_dif"), sem("gate_exp"), sem("xh_hi")
        gu_full, sg_done, hp_done, hh_done, hl_done = (sem(n) for n in ("gu_full", "sg_done", "hp_done", "hh_done", "hl_done"))
        y_full, y_free = sem("y_full"), sem("y_free")
        dve_chain, pool_chain = sem("dve_chain"), sem("pool_chain")
        stored = sem("stored")
        order = schedule()
        norms = [tuple(at) for kind, *at in order if kind == "ln"]

        misc = {}
        ring = {"short": False, 0: 0, 1: 0, 2: 0, 3: 0}

        def misc_take(pe, key):
            bank = len(misc) % 4 if not ring["short"] else 2 + len(misc) % 2
            ring[bank] += 1
            use = ring[bank]
            if use > 1:
                pe.wait_ge(misc_free[bank], use - 1)
            misc[key] = (bank, use)
            return p_misc[:, bank, :], misc_full[bank]

        def misc_wait(eng, key):
            bank, use = misc[key]
            eng.wait_ge(misc_full[bank], use)
            return p_misc[:, bank, :], misc_free[bank]

        def misc_done(eng, key):
            bank, use = misc[key]
            eng.wait_ge(misc_free[bank], use)

        block = ctx.enter_context(nc.Block())

        def head_number(layer, b, h):
            return b * H0 + h if layer == 0 else B * H0 + b * H1 + h

        def group_number(layer, b, g):
            return b * 2 + g if layer == 0 else B * 2 + b * 4 + g

        @block.tensor
        def _(pe):
            def transposes(key, parts):
                ps, full = misc_take(pe, key)
                at = 0
                for src in parts:
                    k, m = src.shape
                    last = pe.transpose(ps[0:m, at:at + k], src, ident[0:k, 0:k])
                    at += k
                last.then_inc(full, 1)

            def context(b):
                if b < 2:
                    pe.wait_ge(ld_c[b], 16)
                if b == 0:
                    pe.wait_ge(const_pe, 1)
                transposes(("cT", b), [raw[:, b * KT + i, :] for i in range(KT)])

            def warm(n):
                pe.wait_ge(warm_set, 1)
                for _ in range(n):
                    pe.matmul(p_o[:, 1, :], warm_in[:, 0:P], warm_in, start=True, stop=True)

            def keys0(b, m):
                if b == 0 and m == 0:
                    pe.wait_ge(wc_split, 1)
                if m == 0:
                    misc_done(pe, ("cT", b))
                ps, full = misc_take(pe, ("k0", b, m))
                for i, (ws, cs) in enumerate(((0, 0), (1, 0), (0, 1))):
                    last = pe.matmul(ps, wc[:, ws, m * P:(m + 1) * P], cT[:, cs, b * C:(b + 1) * C], start=(i == 0), stop=(i == 2))
                last.then_inc(full, 1)

            def values0(b, kt):
                if b == 0 and kt == 0:
                    pe.wait_ge(wc_split, 2)
                ps, full = misc_take(pe, ("v0", b, kt))
                for i, (cs, ws) in enumerate(((0, 0), (0, 1), (1, 0))):
                    last = pe.matmul(ps, cT[:, cs, b * C + kt * P:b * C + (kt + 1) * P], wc[:, ws, H0 * DH0:2 * H0 * DH0],
                                     start=(i == 0), stop=(i == 2))
                last.then_inc(full, 1)

            def xt(kind, b):
                n = norms.index((kind, b))
                pe.wait_ge(ln_xn, n + 1)
                transposes(("xT", kind, b), [xn[:, n % 2, i, :] for i in range(T)])

            def queries0(b, i):
                n = norms.index(("q0", b))
                if b == 0 and i == 0:
                    pe.wait_ge(ld_w0, 16)
                misc_done(pe, ("xT", "q0", b))
                ps, full = misc_take(pe, ("q0", b, i))
                for m in (2 * i, 2 * i + 1):
                    last = pe.matmul(ps[:, (m % 2) * S:(m % 2 + 1) * S], wq0[:, m * P:(m + 1) * P], xT[:, n % 2, :],
                                     start=True, stop=True)
                last.then_inc(full, 1)

            def maxima(layer, b, h):
                u = head_number(layer, b, h)
                if h == 0:
                    stacked = 96 * (b + 1) if layer == 0 else 96 * B + 48 * (b + 1)
                    pe.wait_ge(k_stacked, stacked)
                    pe.wait_ge(q_stacked, stacked)
                    if layer == 1 and b == 1:
                        pe.wait_ge(stack_copied, 16)
                q, k = (qA[:, b % 2, h, :], kA[:, b % 2, h, :]) if layer == 0 else (
                    qS[0:SEL1, b % 2, h, :], kS[0:SEL1, b % 2, h, :])
                for i in range(T):
                    ps, full = misc_take(pe, ("max", layer, b, h, i))
                    pe.matmul(ps, q[:, i * P:(i + 1) * P], k, start=True, stop=True).then_inc(full, 1)

            def rows(layer, b, g):
                last = {misc["max", layer, b, h, i][0]: ("max", layer, b, h, i) for h in range(4 * g, 4 * g + 4) for i in range(T)}
                for key in last.values():
                    misc_done(pe, key)
                transposes(("rows", layer, b, g), [mx[:, b % 2, i, 4 * g:4 * g + 4] for i in range(T)])

            def scores(layer, b, h):
                u = head_number(layer, b, h)
                if h % 4 == 0:
                    pe.wait_ge(rows_set, group_number(layer, b, h // 4) + 1)
                if layer == 0:
                    if b < 2 and h == 0:
                        pe.wait_ge(stack_init, b + 1)
                    pairs = [(kA[:, b % 2, h, :], qA[:, b % 2, h, :]), (kB[:, b % 2, h, :], qB[:, b % 2, h, :])]
                else:
                    pairs = [(kS[:, b % 2, h, :], qS[:, b % 2, h, :])]
                for half in range(2):
                    if u:
                        pe.wait_ge(sc_free[half], u)
                    for j in range(2):
                        kt = 2 * half + j
                        for i, (k, q) in enumerate(pairs):
                            last = pe.matmul(p_sc[:, half, j * S:(j + 1) * S], k[:, kt * P:(kt + 1) * P], q,
                                             start=(i == 0), stop=(i == len(pairs) - 1))
                    last.then_inc(sc_full[half], 1)

            def attend(layer, b, g, c):
                n = group_number(layer, b, g)
                u = head_number(layer, b, 4 * (g + 1))
                if c == 0:
                    pe.wait_ge(sc_free[0], u)
                    pe.wait_ge(sc_free[1], u)
                    if n:
                        pe.wait_ge(o_free, n if layer == 0 or n == 2 * B else n - 1)
                if layer == 0:
                    m = c // 2
                    for kt in (2 * (c % 2), 2 * (c % 2) + 1):
                        for i in range(2):
                            h = 4 * g + 2 * m + i
                            pe.matmul(p_o[64 * i:64 * i + 64, 0, m * S:(m + 1) * S], v0[:, b % 2, kt, h * DH0:(h + 1) * DH0],
                                      probs[:, h % 8, kt * S:(kt + 1) * S], start=(kt == 0), stop=(kt == KT - 1))
                    if c == 3:
                        pe.wait_ge(sums_set, u)
                        if n == 0:
                            pe.wait_ge(const_pe, 2)
                        for j in range(4):
                            last = pe.matmul(p_o[32 * j:32 * j + 32, 1, 0:S], ones[:, :], psums[:, j, :], start=True, stop=True,
                                             tile_position=(0, 32 * j))
                        last.then_inc(av_done, 1)
                else:
                    for j in range(4):
                        h = 4 * g + j
                        last = pe.matmul(p_o[32 * j:32 * j + 32, n % 2, 0:S], v1[:, b % 2, c, h * VW:h * VW + 32],
                                         probs[:, h % 8, c * S:(c + 1) * S], start=(c == 0), stop=(c == KT - 1),
                                         tile_position=(0, 32 * j))
                    if c == 3:
                        last.then_inc(av_done, 1)

            def sums_t(b):
                pe.wait_ge(o_free, 2 * (b + 1))
                transposes(("sT", b), [ssb[:, g, i * P:(i + 1) * P] for i in range(T) for g in range(2)])

            def heads_t(b, i):
                transposes(("oT", b, i), [osb[:, m, i * P:(i + 1) * P] for m in range(M0)])

            def heads_back(b, i):
                misc_done(pe, ("oT", b, i))
                transposes(("aT", b, i), [a0[:, m * P:(m + 1) * P] for m in range(M0)])

            def project0(b, i):
                if b == 0 and i == 0:
                    pe.wait_ge(ld_w1, 16 * 6)
                misc_done(pe, ("aT", b, i))
                ps, full = misc_take(pe, ("y0", b, i))
                for m in range(M0):
                    last = pe.matmul(ps[:, 0:P], aT[:, m * P:(m + 1) * P], wo0[:, m, :], start=(m == 0), stop=(m == M0 - 1))
                last.then_inc(full, 1)

            def up0(b, i):
                n = norms.index(("f", b))
                misc_done(pe, ("xT", "f", b))
                ps, full = misc_take(pe, ("h0", b, i))
                for f in (2 * i, 2 * i + 1):
                    last = pe.matmul(ps[:, (f % 2) * S:(f % 2 + 1) * S], f0w1[:, f * P:(f + 1) * P], xT[:, n % 2, :],
                                     start=True, stop=True)
                last.then_inc(full, 1)

            def down0(b):
                pe.wait_ge(hidden, b + 1)
                ps, full = misc_take(pe, ("z0", b))
                hid = fixed[b // 2][:, 0, :]
                for i in range(T):
                    for f in range(FF):
                        last = pe.matmul(ps[:, i * P:(i + 1) * P], hid[:, f * S + i * P:f * S + (i + 1) * P], f0w2[:, f, :],
                                         start=(f == 0), stop=(f == FF - 1))
                last.then_inc(full, 1)

            def keys1(b):
                if b == 0:
                    pe.wait_ge(ld_w2, 16 * 9)
                ps, full = misc_take(pe, ("k1", b))
                at = 2 * H0 * DH0
                for i, (ws, cs) in enumerate(((0, 0), (1, 0), (0, 1))):
                    last = pe.matmul(ps, wc[:, ws, at:at + P], cT[:, cs, b * C:(b + 1) * C], start=(i == 0), stop=(i == 2))
                last.then_inc(full, 1)

            def values1(b):
                ps, full = misc_take(pe, ("v1", b))
                at = 2 * H0 * DH0 + P
                for kt in range(KT):
                    for i, (cs, ws) in enumerate(((0, 0), (0, 1), (1, 0))):
                        last = pe.matmul(ps[:, kt * P:(kt + 1) * P], cT[:, cs, b * C + kt * P:b * C + (kt + 1) * P], wc[:, ws, at:at + P],
                                         start=(i == 0), stop=(i == 2))
                last.then_inc(full, 1)

            def queries1(b):
                n = norms.index(("q1", b))
                misc_done(pe, ("xT", "q1", b))
                ps, full = misc_take(pe, ("q1", b))
                pe.matmul(ps[:, 0:S], wq1[:, :], xT[:, n % 2, :], start=True, stop=True).then_inc(full, 1)

            def heads_t1(b, i):
                if i == 0:
                    pe.wait_ge(o_free, 2 * B + 4 * (b + 1))
                transposes(("oT1", b, i), [osb[:, g, i * P:(i + 1) * P] for g in range(4)])

            def heads_back1(b):
                misc_done(pe, ("oT1", b, 0))
                misc_done(pe, ("oT1", b, 1))
                transposes(("aT1", b), [a0[:, i * P:(i + 1) * P] for i in range(T)])

            def up1(b):
                misc_done(pe, ("aT1", b))
                ps, full = misc_take(pe, ("h1", b))
                for f in range(2):
                    last = pe.matmul(ps[:, f * S:(f + 1) * S], f1w1[:, f * P:(f + 1) * P], aT[:, 0:S], start=True, stop=True)
                last.then_inc(full, 1)

            def down1(b):
                misc_done(pe, ("h1", b))
                ps, full = misc_take(pe, ("y1", b))
                for i in range(T):
                    for f in range(2):
                        last = pe.matmul(ps[:, i * P:(i + 1) * P], ssb[:, f, i * P:(i + 1) * P], f1w2[:, f, :],
                                         start=(f == 0), stop=(f == 1))
                last.then_inc(full, 1)

            def logits(b):
                n = norms.index(("ex", b))
                misc_done(pe, ("xT", "ex", b))
                ps, full = misc_take(pe, ("logits", b))
                for i in range(T):
                    last = pe.matmul(ps[:, i * E:(i + 1) * E], xT[:, n % 2, i * P:(i + 1) * P], wg[:, :], start=True, stop=True)
                last.then_inc(full, 1)

            def gate_up(n, f):
                half, e = n // E, n % E
                k = n * FF + f
                if f == 0 and e == 0:
                    misc_done(pe, ("xT", "ex", 2 * half))
                    misc_done(pe, ("xT", "ex", 2 * half + 1))
                if f == 0 and half == 0:
                    pe.wait_ge(stage_free, 2 * (e + 1))
                if k == 0:
                    ring["short"] = True
                    for i in range(2):
                        pe.wait_ge(misc_free[i], ring[i])
                        pe.wait_ge(sc_free[i], B * (H0 + H1))
                if k >= 2:
                    pe.wait_ge(hp_done, k - 1)
                for ps, w in ((p_misc, ew[0]), (p_sc, ew[1])):
                    for i, (ws, xs) in enumerate(((0, 0), (0, 1), (1, 0))):
                        last = pe.matmul(ps[:, f % 2, :], w[:, ws, e, f * P:(f + 1) * P], xh[:, xs, half * C:(half + 1) * C],
                                         start=(i == 0), stop=(i == 2))
                last.then_inc(gu_full, 1)

            def down(n, i):
                half, e = n // E, n % E
                if i == 0:
                    if half == 0:
                        pe.wait_ge(stage_free, 2 * E + e + 1)
                    pe.wait_ge(hl_done, FF * (n + 1))
                    if n == 0:
                        pe.wait_ge(o_free, 6 * B)
                    if n >= 2:
                        pe.wait_ge(y_free, n - 1)
                at = 0
                for f in range(FF):
                    for hs, ws in ((0, 0), (0, 1), (1, 0)):
                        last = pe.matmul(p_o[:, n % 2, i * P:(i + 1) * P], hh[:, n % 2, hs, f, i * P:(i + 1) * P],
                                         ew[2][:, ws, e, f * P:(f + 1) * P], start=(at == 0), stop=(at == 3 * FF - 1))
                        at += 1
                if i == 3:
                    last.then_inc(y_full, 1)

            def down_last(f):
                n, e = 2 * E - 1, E - 1
                pe.wait_ge(hl_done, FF * n + f + 1)
                if f == 0:
                    pe.wait_ge(y_free, n - 1)
                for i in range(4):
                    for hs, ws in ((0, 0), (0, 1), (1, 0)):
                        last = pe.matmul(p_o[:, n % 2, i * P:(i + 1) * P], hh[:, n % 2, hs, f, i * P:(i + 1) * P],
                                         ew[2][:, ws, e, f * P:(f + 1) * P], start=(f == i == hs == ws == 0),
                                         stop=(f == FF - 1 and i == 3 and hs == 1))
                if f == FF - 1:
                    last.then_inc(y_full, 1)

            steps = {"dn_last": down_last, "warm": warm, "cT": context, "k0": keys0, "v0": values0, "xT": xt, "q0": queries0, "max": maxima, "rows": rows, "sc": scores,
                     "av": attend, "sT": sums_t, "oT": heads_t, "aT": heads_back, "y0": project0, "up0": up0, "down0": down0,
                     "k1": keys1, "v1": values1, "q1": queries1, "oT1": heads_t1, "aT1": heads_back1, "h1": up1, "y1": down1,
                     "logits": logits, "gu": gate_up, "dn": down}
            for kind, *at in order:
                if kind in steps:
                    steps[kind](*at)

        @block.vector
        def _(dve):
            chain = [0]

            def link(ins):
                chain[0] += 1
                ins.then_inc(dve_chain, 1)
                dve.wait_ge(dve_chain, chain[0])

            def norm(kind, b):
                n = norms.index((kind, b))
                if n < 2:
                    dve.wait_ge(ld_x[n], 16)
                for i in range(T):
                    last = dve.bn_stats(stats[:, i, :], x_sb[:, b * T + i, :])
                link(last)
                for i in range(T):
                    last = dve.bn_aggr(meanvar[:, n % 2, i, :], stats[:, i, :])
                last.then_inc(ln_var, 1)
                dve.wait_ge(ln_var, n + 1)

            def normed(kind, b):
                n = norms.index((kind, b))
                dve.wait_ge(ln_rstd, n + 1)
                if n >= 2:
                    misc_done(dve, ("xT", *norms[n - 2]))
                for i in range(T):
                    last = dve.tensor_scalar(xn[:, n % 2, i, :], x_sb[:, b * T + i, :], meanvar[:, n % 2, i, 0:1],
                                             rstd[:, n % 2, i:i + 1], ALU.subtract, ALU.mult)
                last.then_inc(ln_xn, 1)

            def xt(kind, b):
                if kind == "ex":
                    dve.wait_ge(xh_hi, b + 1)
                    ps, free = misc_wait(dve, ("xT", kind, b))
                    dve.tensor_tensor(xh[:, 1, b * S:(b + 1) * S], ps[:, 0:S], xh[:, 0, b * S:(b + 1) * S], ALU.subtract).then_inc(free, 1)

            def split_w(n):
                cols = slice(0, H0 * DH0) if n == 0 else slice(H0 * DH0, None)
                dve.wait_ge(wc_hi, n + 1)
                dve.tensor_tensor(wc[:, 1, cols], wc_in[:, cols], wc[:, 0, cols], ALU.subtract).then_inc(wc_split, 1)

            def context(b):
                dve.wait_ge(c_hi, b + 1)
                ps, free = misc_wait(dve, ("cT", b))
                cols = slice(b * C, (b + 1) * C)
                dve.tensor_tensor(cT[:, 1, cols], ps[0:CD, :], cT[:, 0, cols], ALU.subtract).then_inc(free, 1)

            def keys0(b, m):
                dve.wait_ge(k_hi, b * M0 + m + 1)
                ps, free = misc_wait(dve, ("k0", b, m))
                dve.tensor_tensor(kx[:, 1, m, :], ps, kx[:, 0, m, :], ALU.subtract).then_inc(free, 1)

            def queries0(b, i):
                dve.wait_ge(q_hi, b * 2 + i + 1)
                ps, free = misc_wait(dve, ("q0", b, i))
                dve.tensor_tensor(qx[:, 1, 2 * i:2 * i + 2, :].rearrange("p m n -> p (m n)"), ps,
                                  qx[:, 0, 2 * i:2 * i + 2, :].rearrange("p m n -> p (m n)"), ALU.subtract).then_inc(free, 1)

            def maxima(layer, b, h):
                for i in range(T):
                    ps, free = misc_wait(dve, ("max", layer, b, h, i))
                    dve.tensor_reduce(mx[:, b % 2, i, h:h + 1], ps, AX_X, ALU.max).then_inc(free, 1)

            def init(n):
                if n < 2:
                    dve.memset(kB[SEL0:P, n, :, :].rearrange("p h k -> p (h k)").bitcast(F32), 0.0).then_inc(zero_kb, 1)
                    dve.memset(qB[SEL0:P, n, :, :].rearrange("p h k -> p (h k)").bitcast(F32), 0.0).then_inc(zero_kb, 1)
                    dve.wait_ge(zero_kb, 2 * n + 2)

            def rows(layer, b, g):
                heads = slice(4 * g, 4 * g + 4)
                dst = qB[SEL0:SEL0 + 4, b % 2, heads, :] if layer == 0 else qS[SEL1:SEL1 + 4, b % 2, heads, :]
                misc_done(dve, ("rows", layer, b, g))
                dve.tensor_copy(dst, mrow[:, :].unsqueeze(1).broadcast_to([4, 4, S])).then_inc(rows_set, 1)
                dve.wait_ge(rows_set, group_number(layer, b, g) + 1)

            def sums_t(b):
                ps, free = misc_wait(dve, ("sT", b))
                dve.reciprocal(rden[:, :, 0:H0], ps.rearrange("p (i h r) -> p i h r", i=T, r=32)[:, :, :, 0]).then_inc(free, 1)
                misc_done(dve, ("sT", b))

            def heads_t(b, i):
                ps, free = misc_wait(dve, ("oT", b, i))
                dve.tensor_tensor(a0[:, :].rearrange("p (h d) -> p h d", h=H0), ps.rearrange("p (h d) -> p h d", h=H0),
                                  rden[:, i, 0:H0].unsqueeze(2).broadcast_to([P, H0, DH0]), ALU.mult).then_inc(free, 1)

            def add_to_x(b, key, bias, tiles=slice(0, T)):
                ps, free = misc_wait(dve, key)
                n = tiles.stop - tiles.start
                tokens, biased = x_sb[:, b * T:(b + 1) * T, :][:, tiles, :], ytmp[:, tiles, :]
                dve.tensor_tensor(biased, ps[:, 0:n * P].rearrange("p (a b) -> p a b", a=n),
                                  bias.unsqueeze(1).broadcast_to([P, n, P]), ALU.add).then_inc(free, 1)
                misc_done(dve, key)
                link(dve.tensor_tensor(tokens, tokens, biased, ALU.add))

            def project0(b, i):
                if b == 0 and i == 0:
                    dve.wait_ge(ld_w1, 16 * 6)
                    dve.tensor_scalar(f0b1x[:, :], f0b1[:, :], FIX, None, ALU.mult).then_inc(f0b1_set, 1)
                add_to_x(b, ("y0", b, i), bo0[:, :], slice(i, i + 1))

            def rounded(b):
                N, F, G, Y1 = (fixed[b // 2][:, i, :] for i in range(4))
                for i in range(2):
                    misc_done(dve, ("h0", b, i))
                link(dve.tensor_scalar(N, N, MAGIC, MAGIC, ALU.add, ALU.subtract))
                link(dve.tensor_scalar(Y1, N, -4 * FIX, 4 * FIX - 1, ALU.max, ALU.min))

            def floor(b):
                N, F, G, Y1 = (fixed[b // 2][:, i, :] for i in range(4))
                link(dve.tensor_scalar(G, Y1, -(STEP - 1) / 2, BREAK, ALU.add, ALU.add))
                dve.scalar_tensor_tensor(F, G, BREAK, Y1, ALU.subtract, ALU.subtract).then_inc(breaks, 1)
                dve.wait_ge(breaks, b + 1)

            def slope(b):
                N, F, G, Y1 = (fixed[b // 2][:, i, :] for i in range(4))
                dve.wait_ge(nodes, 2 * (b + 1))
                link(dve.tensor_tensor(Y1, Y1, G, ALU.subtract))
                link(dve.scalar_tensor_tensor(F, F, -FIX / STEP, Y1, ALU.mult, ALU.mult))

            def interp(b):
                N, F, G, Y1 = (fixed[b // 2][:, i, :] for i in range(4))
                link(dve.scalar_tensor_tensor(G, G, FIX, F, ALU.mult, ALU.add))

            def identity(b):
                N, F, G, Y1 = (fixed[b // 2][:, i, :] for i in range(4))
                link(dve.tensor_scalar(G, G, MAGIC, MAGIC + 4 * FIX - 1, ALU.add, ALU.subtract))
                dve.scalar_tensor_tensor(N, N, 4 * FIX - 1, G, ALU.max, ALU.add).then_inc(hidden, 1)
                dve.wait_ge(hidden, b + 1)

            def add0(b):
                ps, free = misc_wait(dve, ("z0", b))
                flat = ytmp[:, :, :].rearrange("p a b -> p (a b)")
                dve.scalar_tensor_tensor(ytmp[:, :, :], ps[:, 0:T * P].rearrange("p (a b) -> p a b", a=T), 1.0 / FIX,
                                         f0b2[:, :].unsqueeze(1).broadcast_to([P, T, P]), ALU.mult, ALU.add).then_inc(free, 1)
                misc_done(dve, ("z0", b))
                link(dve.tensor_scalar(flat, flat, FIX, MAGIC, ALU.mult, ALU.add))
                link(dve.tensor_scalar(flat, flat, MAGIC, 1.0 / FIX, ALU.subtract, ALU.mult))
                link(dve.tensor_tensor(x_sb[:, b * T:(b + 1) * T, :], x_sb[:, b * T:(b + 1) * T, :], ytmp[:, :, :], ALU.add))

            def keys1(b):
                dve.wait_ge(k_hi, B * M0 + b + 1)
                ps, free = misc_wait(dve, ("k1", b))
                dve.scalar_tensor_tensor(kx[:, 1, 0, :], ps, bk1[:, 0:1], kx[:, 0, 0, :], ALU.add, ALU.subtract).then_inc(free, 1)

            def values1(b):
                ps, free = misc_wait(dve, ("v1", b))
                if b == 0:
                    dve.wait_ge(stack_init, 6)
                for kt in range(KT):
                    last = dve.tensor_tensor(v1[:, b % 2, kt, 0:VW * H1].rearrange("p (h c) -> p h c", c=VW)[:, :, 0:DH1],
                                             ps[:, kt * P:(kt + 1) * P].rearrange("p (h d) -> p h d", h=H1),
                                             bv1[:, :].rearrange("p (h d) -> p h d", h=H1), ALU.add)
                last.then_inc(free, 1)

            def queries1(b):
                dve.wait_ge(q_hi, 2 * B + b + 1)
                ps, free = misc_wait(dve, ("q1", b))
                dve.scalar_tensor_tensor(qx[:, 1, 0, :], ps[:, 0:S], bq1[:, 0:1], qx[:, 0, 0, :], ALU.add, ALU.subtract).then_inc(free, 1)

            def heads_t1(b, i):
                ps, free = misc_wait(dve, ("oT1", b, i))
                cols = ps.rearrange("p (h r) -> p h r", r=32)
                link(dve.reciprocal(rden[:, i, :], cols[:, :, DH1]))
                dve.tensor_tensor(a0[:, i * P:(i + 1) * P].rearrange("p (h d) -> p h d", h=H1), cols[:, :, 0:DH1],
                                  rden[:, i, :].unsqueeze(2).broadcast_to([P, H1, DH1]), ALU.mult).then_inc(free, 1)

            def add1(b):
                add_to_x(b, ("y1", b), f1b2[:, :])

            def logits(b):
                ps, free = misc_wait(dve, ("logits", b))
                dve.tensor_copy(lg[:, 0, b * T:(b + 1) * T, :], ps[:, 0:T * E].rearrange("p (t e) -> p t e", t=T)).then_inc(free, 1)
                misc_done(dve, ("logits", b))

            def route(half):
                NT = B * T // 2
                r = slice(half * NT, half * NT + NT)
                logit, dif = (lg[:, i, r, :] for i in range(2))
                top = gs[:, 0, r]

                def wide(v):
                    return v.unsqueeze(2).broadcast_to([P, NT, E])

                link(dve.tensor_reduce(top, logit, AX_X, ALU.max))
                dve.tensor_tensor(dif, logit, wide(top), ALU.subtract).then_inc(gate_dif, 1)

            def shares(half):
                NT = B * T // 2
                r = slice(half * NT, half * NT + NT)
                ex, prob = (lg[:, i, r, :] for i in (2, 3))
                norm_, inv = (gs[:, i, r] for i in (1, 2))
                dve.wait_ge(gate_exp, half + 1)
                link(dve.tensor_reduce(norm_, ex, AX_X, ALU.add))
                link(dve.reciprocal(inv, norm_))
                link(dve.tensor_tensor(prob, ex, inv.unsqueeze(2).broadcast_to([P, NT, E]), ALU.mult))

            def compare(half):
                NT = B * T // 2
                prob = lg[:, 3, half * NT:(half + 1) * NT, :]
                for i in range(NT):
                    this = prob[:, i, :].unsqueeze(2).broadcast_to([P, E, E])
                    other = prob[:, i, :].unsqueeze(1).broadcast_to([P, E, E])
                    dve.tensor_tensor(cmp_[:, 0, half * NT + i, :, :], other, this, ALU.is_gt)
                    last = dve.tensor_tensor(cmp_[:, 1, half * NT + i, :, :], other, this, ALU.is_equal)
                link(last)

            def rank(half):
                NT = B * T // 2
                r = slice(half * NT, half * NT + NT)
                picked = lg[:, 4, r, :]
                great, same = (cmp_[:, i, r, :, :].rearrange("p t e f -> p t (e f)") for i in range(2))
                link(dve.tensor_tensor(same, same, tri[:, :, :].rearrange("p e f -> p (e f)").unsqueeze(1).broadcast_to([P, NT, E * E]), ALU.mult))
                link(dve.tensor_tensor(great, great, same, ALU.add))
                link(dve.tensor_reduce(picked, cmp_[:, 0, r, :, :], AX_X, ALU.add))

            def best(half):
                NT = B * T // 2
                r = slice(half * NT, half * NT + NT)
                prob, picked = (lg[:, i, r, :] for i in (3, 4))
                top, norm_, inv = (gs[:, i, r] for i in range(3))
                link(dve.scalar_tensor_tensor(picked, picked, 1.5, prob, ALU.is_lt, ALU.mult))
                link(dve.tensor_reduce(top, picked, AX_X, ALU.add))
                link(dve.tensor_scalar(norm_, top, 1e-8, None, ALU.add))
                link(dve.reciprocal(inv, norm_))
                link(dve.tensor_tensor(comb[:, r, :], picked, inv.unsqueeze(2).broadcast_to([P, NT, E]), ALU.mult))

            def product(k):
                dve.wait_ge(sg_done, k + 1)
                if k >= 2:
                    dve.wait_ge(hl_done, k - 1)
                dve.tensor_tensor(hp[:, k % 2, :], sg[:, k % 2, :], p_sc[:, k % 2, :], ALU.mult).then_inc(hp_done, 1)

            def low(k):
                n, f = k // FF, k % FF
                dve.wait_ge(hh_done, k + 1)
                dve.tensor_tensor(hh[:, n % 2, 1, f, :], hp[:, k % 2, :], hh[:, n % 2, 0, f, :], ALU.subtract).then_inc(hl_done, 1)

            def mix(n):
                half, e = n // E, n % E
                dve.wait_ge(y_full, n + 1)
                if n:
                    dve.wait_ge(y_free, n)
                for i in range(4):
                    tt = half * 4 + i
                    last = dve.scalar_tensor_tensor(x_sb[:, tt, :], p_o[:, n % 2, i * P:(i + 1) * P], comb[:, tt, e:e + 1],
                                                    x_sb[:, tt, :], ALU.mult, ALU.add)
                last.then_inc(y_free, 1)

            def activate(n, f):
                k = n * FF + f
                if n < 2 * E:
                    product(k)
                if k:
                    low(k - 1)
                if f == 3 and n:
                    mix(n - 1)

            dve.memset(warm_in.bitcast(F32), 0.0).then_inc(warm_set, 1)
            steps = {"split_w": split_w, "cT": context, "ln": norm, "xn": normed, "xT": xt, "k0": keys0, "q0": queries0, "init": init, "max": maxima, "rows": rows, "sT": sums_t, "oT": heads_t,
                     "y0": project0, "round": rounded, "floor": floor, "slope": slope, "interp": interp, "ident": identity, "down0": add0,
                     "k1": keys1, "v1": values1, "q1": queries1, "oT1": heads_t1, "y1": add1, "logits": logits, "route": route, "shares": shares, "compare": compare, "rank": rank,
                     "best": best, "act": activate, "mix": mix}
            for kind, *at in order:
                if kind in steps:
                    steps[kind](*at)

        @block.scalar
        def _(act):
            def copy_out(dst, key, src=lambda ps: ps):
                ps, free = misc_wait(act, key)
                act.copy(dst, src(ps)).then_inc(free, 1)

            def split_w(n):
                cols = slice(0, H0 * DH0) if n == 0 else slice(H0 * DH0, None)
                act.wait_ge(*((ld_wk0, 16) if n == 0 else (ld_wc, 48)))
                act.copy(wc[:, 0, cols], wc_in[:, cols]).then_inc(wc_hi, 1)

            def context(b):
                ps, _free = misc_wait(act, ("cT", b))
                act.copy(cT[:, 0, b * C:(b + 1) * C], ps[0:CD, :]).then_inc(c_hi, 1)

            def keys0(b, m):
                if b and m == 0:
                    act.wait_ge(k_stacked, 96 * b)
                ps, _free = misc_wait(act, ("k0", b, m))
                act.copy(kx[:, 0, m, :], ps).then_inc(k_hi, 1)

            def values0(b, kt):
                copy_out(v0[:, b % 2, kt, :], ("v0", b, kt))

            def xt(kind, b):
                n = norms.index((kind, b))
                if kind != "ex":
                    copy_out(xT[:, n % 2, :], ("xT", kind, b), lambda ps: ps[:, 0:S])
                else:
                    ps, _free = misc_wait(act, ("xT", kind, b))
                    act.copy(xT[:, n % 2, :], ps[:, 0:S])
                    act.copy(xh[:, 0, b * S:(b + 1) * S], ps[:, 0:S]).then_inc(xh_hi, 1)

            def queries0(b, i):
                if b and i == 0:
                    act.wait_ge(q_stacked, 96 * b)
                ps, _free = misc_wait(act, ("q0", b, i))
                act.copy(qx[:, 0, 2 * i:2 * i + 2, :].rearrange("p m n -> p (m n)"), ps).then_inc(q_hi, 1)

            def rows(layer, b, g):
                n = group_number(layer, b, g)
                if n:
                    act.wait_ge(rows_set, n)
                copy_out(mrow[:, :], ("rows", layer, b, g), lambda ps: ps[0:4, 0:S])

            def softmax(layer, b, h):
                u = head_number(layer, b, h)
                n = group_number(layer, b, h // 4)
                if u == 2:
                    act.wait_ge(wc_split, 2)
                for half in range(2):
                    act.wait_ge(sc_full[half], u + 1)
                    if half == 0 and n > 1:
                        act.wait_ge(av_done, n - 1)
                    act.activation(probs[:, h % 8, half * 512:(half + 1) * 512], p_sc[:, half, :], ACT.Exp,
                                   scale=(DH0 if layer == 0 else DH1) ** -0.5).then_inc(sc_free[half], 1)

            def outputs(layer, b, g, c):
                if c < 3:
                    return
                n = group_number(layer, b, g)
                act.wait_ge(av_done, n + 1)
                if layer == 0:
                    act.copy(osb[:, 2 * g:2 * g + 2, :].rearrange("p m n -> p (m n)"), p_o[:, 0, :])
                    act.copy(ssb[:, g, :], p_o[:, 1, 0:S]).then_inc(o_free, 1)
                else:
                    act.copy(osb[:, g, :], p_o[:, n % 2, 0:S]).then_inc(o_free, 1)

            def heads_back(b, i):
                copy_out(aT[:, :], ("aT", b, i))

            def up0(b, i):
                if b == 0 and i == 0:
                    act.wait_ge(f0b1_set, 1)
                ps, free = misc_wait(act, ("h0", b, i))
                for f in (2 * i, 2 * i + 1):
                    last = act.activation(fixed[b // 2][:, 0, f * S:(f + 1) * S], ps[:, (f % 2) * S:(f % 2 + 1) * S], ACT.Identity,
                                          bias=f0b1x[:, f:f + 1], scale=FIX)
                last.then_inc(free, 1)

            def nodes_at(b):
                G, Y1 = (fixed[b // 2][:, i, :] for i in (2, 3))
                act.wait_ge(breaks, b + 1)
                act.activation(Y1, G, ACT.Gelu, bias=node_bias[:, 1:2], scale=1 / FIX).then_inc(nodes, 1)
                act.wait_ge(nodes, 2 * b + 1)
                act.activation(G, G, ACT.Gelu, bias=node_bias[:, 0:1], scale=1 / FIX).then_inc(nodes, 1)

            def keys1(b):
                if b == 0:
                    act.wait_ge(k_stacked, 96 * B)
                else:
                    act.wait_ge(k_bounced, 16 * b)
                ps, _free = misc_wait(act, ("k1", b))
                act.activation(kx[:, 0, 0, :], ps, ACT.Identity, bias=bk1[:, 0:1]).then_inc(k_hi, 1)

            def queries1(b):
                if b == 0:
                    act.wait_ge(q_stacked, 96 * B)
                else:
                    act.wait_ge(q_bounced, 16 * b)
                ps, _free = misc_wait(act, ("q1", b))
                act.activation(qx[:, 0, 0, :], ps[:, 0:S], ACT.Identity, bias=bq1[:, 0:1]).then_inc(q_hi, 1)

            def heads_back1(b):
                copy_out(aT[:, 0:S], ("aT1", b), lambda ps: ps[:, 0:S])

            def up1(b):
                ps, free = misc_wait(act, ("h1", b))
                act.activation(ssb[:, 0, :], ps[:, 0:S], ACT.Relu, bias=f1b1[:, 0:1])
                act.activation(ssb[:, 1, :], ps[:, S:2 * S], ACT.Relu, bias=f1b1[:, 1:2]).then_inc(free, 1)

            def activate(n, f):
                k = n * FF + f
                if n < 2 * E:
                    if k == 0:
                        act.wait_ge(av_done, 6 * B)
                    act.wait_ge(gu_full, k + 1)
                    act.activation(sg[:, k % 2, :], p_misc[:, k % 2, :], ACT.Silu).then_inc(sg_done, 1)
                if k:
                    last_n, last_f = (k - 1) // FF, (k - 1) % FF
                    act.wait_ge(hp_done, k)
                    if last_n >= 2 and last_f == 0:
                        act.wait_ge(y_full, last_n - 1)
                    act.copy(hh[:, last_n % 2, 0, last_f, :], hp[:, (k - 1) % 2, :]).then_inc(hh_done, 1)

            steps = {"split_w": split_w, "cT": context, "k0": keys0, "v0": values0, "xT": xt, "q0": queries0, "rows": rows, "sc": softmax, "av": outputs,
                     "aT": heads_back, "up0": up0, "nodes": nodes_at, "k1": keys1, "q1": queries1, "aT1": heads_back1, "h1": up1,
                     "act": activate}
            for kind, *at in order:
                if kind in steps:
                    steps[kind](*at)

        @block.gpsimd
        def _(pool):
            chain = [0]

            def link(ins):
                chain[0] += 1
                ins.then_inc(pool_chain, 1)
                pool.wait_ge(pool_chain, chain[0])

            def norm(kind, b):
                n = norms.index((kind, b))
                pool.wait_ge(ln_var, n + 1)
                link(pool.tensor_scalar(veps[:, n % 2, :], meanvar[:, n % 2, :, 1], EPS, None, ALU.add))
                pool.tensor_tensor(rstd[:, n % 2, :], veps[:, n % 2, :], mhalf[:, :], ALU.pow).then_inc(ln_rstd, 1)
                pool.wait_ge(ln_rstd, n + 1)

            def select(heads):
                link(pool.affine_select(out=heads, in_=heads, compare_op=ALU.not_equal, fill=-1.0, base=0,
                                        pattern=[[-1, 4], [0, C]], channel_multiplier=1))

            def init(n):
                if n < 2:
                    pool.wait_ge(zero_kb, 2 * n + 1)
                    for g in range(H0 // 4):
                        select(kB[SEL0:P, n, 4 * g:4 * g + 4, :])
                elif n < 4:
                    link(pool.memset(qS[:, n - 2, :, :].rearrange("p h k -> p (h k)").bitcast(F32), 0.0))
                elif n == 4:
                    link(pool.memset(tri[:, :, :], 1.0))
                    link(pool.affine_select(out=tri[:, :, :], in_=tri[:, :, :], compare_op=ALU.is_gt, fill=0.0, base=0,
                                            pattern=[[1, E], [-1, E]], channel_multiplier=0))
                    link(pool.memset(kS[:, 0, :, :].rearrange("p h k -> p (h k)").bitcast(F32), 0.0))
                    for g in range(H1 // 4):
                        select(kS[SEL1:P, 0, 4 * g:4 * g + 4, :])
                else:
                    pool.wait_ge(av_done, 2 * (B - 1))
                    link(pool.memset(v1, 0.0))
                    for b in range(2):
                        link(pool.memset(v1[:, b, :, 0:VW * H1].rearrange("p k (h c) -> p k h c", c=VW)[:, :, :, DH1], 1.0))
                pool.sem_inc(stack_init, 1)

            def sums(b, h):
                u = head_number(0, b, h)
                n = group_number(0, b, h // 4)
                pool.wait_ge(sc_free[0], u + 1)
                pool.wait_ge(sc_free[1], u + 1)
                if n and h % 4 == 0:
                    pool.wait_ge(av_done, n)
                tiles = [probs[:, h % 8, kt * S:(kt + 1) * S] for kt in range(KT)]
                link(pool.tensor_tensor(psums[:, h % 4, :], tiles[0], tiles[1], ALU.add))
                link(pool.tensor_tensor(psums[:, h % 4, :], psums[:, h % 4, :], tiles[2], ALU.add))
                pool.tensor_tensor(psums[:, h % 4, :], psums[:, h % 4, :], tiles[3], ALU.add).then_inc(sums_set, 1)
                pool.wait_ge(sums_set, u + 1)

            def route(half):
                r = slice(half * B * T // 2, (half + 1) * B * T // 2)
                pool.wait_ge(gate_dif, half + 1)
                pool.tensor_tensor(lg[:, 2, r, :], euler[:, :].unsqueeze(2).broadcast_to([P, B * T // 2, E]), lg[:, 1, r, :],
                                   ALU.pow).then_inc(gate_exp, 1)
                pool.wait_ge(gate_exp, half + 1)

            def split(c):
                w, e = (c % 2, c // 2) if c < 2 * E else (2, c - 2 * E)
                pool.wait_ge(ld_stage[c % 2], 16 * (c // 2 + 1))
                link(pool.tensor_copy(ew[w][:, 0, e, :], stage[:, c % 2, :]))
                pool.tensor_tensor(ew[w][:, 1, e, :], stage[:, c % 2, :], ew[w][:, 0, e, :], ALU.subtract).then_inc(stage_free, 1)
                pool.wait_ge(stage_free, c + 1)

            link(pool.memset(ident[:, :], 0.0))
            link(pool.affine_select(out=ident[:, :], in_=ident[:, :], compare_op=ALU.not_equal, fill=1.0, base=0,
                                    pattern=[[-1, P]], channel_multiplier=1))
            pool.sem_inc(const_pe, 1)
            link(pool.memset(mhalf[:, :], -0.5))
            link(pool.memset(node_bias[:, 0:1], -BREAK / FIX))
            link(pool.memset(node_bias[:, 1:2], (STEP - BREAK) / FIX))
            link(pool.memset(ones[:, :], 1.0))
            link(pool.memset(euler[:, :], 2.718281828459045))
            pool.sem_inc(const_pe, 1)
            steps = {"ln": norm, "sum": sums, "init": init, "route": route, "split": split}
            for kind, *at in order:
                if kind in steps:
                    steps[kind](*at)

        @block.sync
        def _(sp):
            def row(v):
                return v.rearrange("(a d) -> a d", a=1).partition_broadcast(P)

            ctx_in = t["ctx_768"].rearrange("b (k p) d -> p b k d", p=P)
            x_in = t["x"].rearrange("b (i p) d -> p b i d", p=P)
            sp.dma_start(raw[:, 0:KT, :], ctx_in[:, 0, :, :]).then_inc(ld_c[0], 16)
            sp.dma_start(wc_in[:, 0:H0 * DH0], t["L0_xattn_Wk"]).then_inc(ld_wk0, 16)
            sp.dma_start(x_sb[:, 0:T, :], x_in[:, 0, :, :]).then_inc(ld_x[0], 16)
            sp.dma_start(wq0[:, :], t["L0_xattn_Wq"]).then_inc(ld_w0, 16)
            sp.dma_start(wc_in[:, H0 * DH0:2 * H0 * DH0], t["L0_xattn_Wv"]).then_inc(ld_wc, 16)
            for i, name in enumerate(("L1_xattn_Wk", "L1_xattn_Wv")):
                at = 2 * H0 * DH0 + i * P
                sp.dma_start(wc_in[:, at:at + P], t[name]).then_inc(ld_wc, 16)
            sp.dma_start(raw[:, KT:, :], t["ctx_768"][1:B].rearrange("b (k p) d -> p (b k) d", p=P)).then_inc(ld_c[1], 16)
            sp.dma_start(x_sb[:, T:, :], t["x"][1:B].rearrange("b (i p) d -> p (b i) d", p=P)).then_inc(ld_x[1], 16)

            def stack0(b):
                for src, what, landed, a, bb in ((kx, "k0", k_stacked, kA, kB), (qx, "q0", q_stacked, qA, qB)):
                    for i in range(M0 if what == "k0" else 2):
                        misc_done(sp, (what, b, i))
                    if b >= 2:
                        sp.wait_ge(sc_full[1], head_number(0, b - 1, 0))
                    for i in range(2):
                        rows = slice(64 * i, 64 * i + 64)
                        low = 0 if what == "k0" else 1
                        sp.dma_start(a[0:64, b % 2, i::2, :], src[rows, 0, :, :]).then_inc(landed, 16)
                        sp.dma_start(a[64:128, b % 2, i::2, :], src[rows, low, :, :]).then_inc(landed, 16)
                        sp.dma_start(bb[0:64, b % 2, i::2, :], src[rows, 1 - low, :, :]).then_inc(landed, 16)

            def bounce(b):
                for src, key, bounced, scr in ((kx, "k1", k_bounced, dk), (qx, "q1", q_bounced, dq)):
                    misc_done(sp, (key, b))
                    sp.dma_start(scr[b], src[:, :, 0, :]).then_inc(bounced, 16)

            def stack1(b):
                for key, bounced, scr, dst, landed, parts in (
                        ("k1", k_bounced, dk, kS, k_stacked, (0, 1, 0)), ("q1", q_bounced, dq, qS, q_stacked, (0, 0, 1))):
                    sp.wait_ge(bounced, 16 * (b + 1))
                    if key == "k1":
                        sp.wait_ge(stack_init, 5)
                        if b >= 2:
                            sp.wait_ge(sc_full[1], head_number(1, b - 1, 0))
                    view = scr[b].rearrange("(h d) s n -> s d h n", d=DH1)
                    for i, part in enumerate(parts):
                        sp.dma_start(dst[DH1 * i:DH1 * (i + 1), b % 2, :, :], view[part]).then_inc(landed, 16)

            def zeros():
                misc_done(sp, ("z0", 1))
                sp.wait_ge(stack_init, 5)
                sp.dma_start(kS[3 * DH1:P, 1, :, :], kS[3 * DH1:P, 0, :, :]).then_inc(stack_copied, 16)

            experts = [t["L1_ffn_W1"], t["L1_ffn_W3"], t["L1_ffn_W2"].rearrange("e (f p) d -> e p f d", p=P)]

            def stage_in(c):
                w, e = (c % 2, c // 2) if c < 2 * E else (2, c - 2 * E)
                if c == 0:
                    sp.wait_ge(av_done, 2 * B)
                if c == 2 * E:
                    misc_done(sp, ("z0", B - 1))
                if c >= 2:
                    sp.wait_ge(stage_free, c - 1)
                dst = stage[:, c % 2, :]
                if w == 2:
                    dst = dst.rearrange("p (f d) -> p f d", f=FF)
                sp.dma_start(dst, experts[w][e]).then_inc(ld_stage[c % 2], 16)

            def rest_of_weights(n):
                if n != 1:
                    return
                sp.dma_start(wo0[:, :, :], t["L0_xattn_Wo"].rearrange("(m p) n -> p m n", p=P)).then_inc(ld_w1, 16)
                sp.dma_start(f0w1[:, :], t["L0_ffn_w1"]).then_inc(ld_w1, 16)
                sp.dma_start(f0w2[:, :, :], t["L0_ffn_w2"].rearrange("(m p) n -> p m n", p=P)).then_inc(ld_w1, 16)
                sp.dma_start(f0b1[:, :], t["L0_ffn_b1"]).then_inc(ld_w1, 16)
                sp.dma_start(bo0[:, :], row(t["L0_xattn_bo"])).then_inc(ld_w1, 16)
                sp.dma_start(f0b2[:, :], row(t["L0_ffn_b2"])).then_inc(ld_w1, 16)
                for dst, src in ((wq1, "L1_xattn_Wq"), (f1w1, "L1_xattn_W1"),
                                 (wg, "L1_ffn_Wg"), (f1b1, "L1_xattn_b1"), (bq1, "L1_xattn_bq"), (bk1, "L1_xattn_bk")):
                    sp.dma_start(dst[:, :], t[src]).then_inc(ld_w2, 16)
                sp.dma_start(f1w2[:, :, :], t["L1_xattn_W2"].rearrange("(m p) n -> p m n", p=P)).then_inc(ld_w2, 16)
                sp.dma_start(bv1[:, :], row(t["L1_xattn_bv"])).then_inc(ld_w2, 16)
                sp.dma_start(f1b2[:, :], row(t["L1_xattn_b2"])).then_inc(ld_w2, 16)

            steps = {"stack0": stack0, "zeros": zeros, "bounce": bounce, "stack1": stack1, "stage": stage_in, "init": rest_of_weights}
            for kind, *at in order:
                if kind in steps:
                    steps[kind](*at)
            for half in range(2):
                sp.wait_ge(y_free, E * (half + 1))
                sp.dma_start(out.rearrange("b (i p) d -> p (b i) d", p=P)[:, half * 4:half * 4 + 4, :],
                             x_sb[:, half * 4:half * 4 + 4, :]).then_inc(stored, 16)
            sp.wait_ge(stored, 32)


_INS = ['x', 'ctx_768', 'L0_xattn_Wq', 'L0_xattn_Wk', 'L0_xattn_Wv', 'L0_xattn_Wo', 'L0_xattn_bo', 'L0_ffn_w1', 'L0_ffn_b1',
        'L0_ffn_w2', 'L0_ffn_b2', 'L1_xattn_Wq', 'L1_xattn_bq', 'L1_xattn_Wk', 'L1_xattn_bk', 'L1_xattn_Wv', 'L1_xattn_bv',
        'L1_xattn_W1', 'L1_xattn_b1', 'L1_xattn_W2', 'L1_xattn_b2', 'L1_ffn_Wg', 'L1_ffn_W1', 'L1_ffn_W2', 'L1_ffn_W3']


def kernel(**inputs):
    import numpy as _np
    import concourse.bacc as _bacc
    from concourse import mybir as _mybir
    from concourse.bass_utils import run_bass_kernel_spmd as _run

    nc = _bacc.Bacc("TRN2", target_bir_lowering=False, num_devices=1)
    arrays, aps = {}, {}
    for name in _INS:
        a = _np.asarray(inputs[name])
        if name in ("L0_ffn_b1", "L1_xattn_b1", "L1_xattn_bq", "L1_xattn_bk"):
            a = a.reshape(-1, P).T
        a = _np.ascontiguousarray(a)
        arrays[f"in_{name}_dram"] = a
        aps[name] = nc.dram_tensor(f"in_{name}_dram", a.shape, _mybir.dt.from_np(a.dtype), kind="ExternalInput").ap()
    out = nc.dram_tensor("out_dram", (B, S, P), _mybir.dt.float32, kind="ExternalOutput").ap()
    build(nc, aps, out)
    r = _run(nc, [arrays], core_ids=[0])
    return r.results[0]["out_dram"]
```
